# Optimizing a Trainium2 kernel written in Bass

```python
import numpy as np
import jax
import jax.numpy as jnp

def _softmax(x, axis=-1):
    return jax.nn.softmax(x, axis=axis)

def _gelu(x):
    return jax.nn.gelu(x, approximate=True)

def _silu(x):
    return jax.nn.silu(x)

def _sigmoid(x):
    return jax.nn.sigmoid(x)

def _layernorm(x, axis=-1, eps=1e-05):
    m = jnp.mean(x, axis=axis, keepdims=True)
    v = jnp.var(x, axis=axis, keepdims=True)
    return (x - m) / jnp.sqrt(v + eps)

def _scatter_add(tgt, idx, src, axis=0):
    return tgt.at[idx].add(src)

def _segment_sum(src, seg, n):
    return jax.ops.segment_sum(src, seg, n)
kernel_name = 'mk_flamingo_gated_d1_seqx_r8_43b7f8'

def setup_inputs(seed: int=0):
    np.random.seed(seed)
    _w = jnp.asarray

    def _rec_inputs():
        import jax
        import jax.numpy as jnp
        _rk = jax.random.key(seed)
        x = -0.0002928 + 1 * jax.random.normal(jax.random.fold_in(_rk, 1), (32, 100, 128), jnp.float32)
        _lenS = 100 - jax.random.randint(jax.random.fold_in(_rk, 7), (32,), 0, max(1, 100 // 4) + 1, jnp.int32)
        _lenS2 = 1444 - jax.random.randint(jax.random.fold_in(_rk, 8), (32,), 0, max(1, 1444 // 4) + 1, jnp.int32)
        _ctx_512P = jax.random.normal(jax.random.fold_in(_rk, 11), (32, 16, 64), jnp.float32)
        _ctx_512c = jax.random.dirichlet(jax.random.fold_in(_rk, 511), 0.3 * jnp.ones((16,), jnp.float32), (32, 1444))
        _ctx_512t = jnp.einsum('bsk,bkd->bsd', _ctx_512c, _ctx_512P)
        _ctx_512t = _ctx_512t * jax.lax.rsqrt(jnp.mean(jnp.square(_ctx_512t)) + 1e-12) * 0.953939
        ctx_512 = -0.000514642 + 1.00011 * (_ctx_512t + 0.3 * jax.random.normal(jax.random.fold_in(_rk, 611), (32, 1444, 64), jnp.float32))
        _g = jax.random.normal(jax.random.fold_in(_rk, 9001), (2, 1), jnp.float32)
        _g = jnp.sign(_g) * jnp.maximum(jnp.abs(_g), 1.0) + (_g == 0) * 1.0
        g_xattn = _g[0]
        g_ffn = _g[1]
        return (x, ctx_512, g_xattn, g_ffn)
    x, ctx_512, g_xattn, g_ffn = _rec_inputs()

    def _L0_xattn_setup():
        import jax, jax.numpy as jnp
        import numpy as np
        DIM = 128
        LATENT_DIM = 64
        NUM_HEADS = 16
        HEAD_DIM = DIM // NUM_HEADS
        SCALE = HEAD_DIM ** (-0.5)
        key = jax.random.key(seed)
        k1, k2, k3, k4, k5 = jax.random.split(key, 5)
        B, xN, zN = (2, 256, 256)
        x = jax.random.normal(k1, (B, xN, DIM), dtype=jnp.float32)
        z = jax.random.normal(k2, (B, zN, LATENT_DIM), dtype=jnp.float32)
        Wq = jax.random.normal(k3, (DIM, DIM), dtype=jnp.float32) * DIM ** (-0.5)
        Wkv = jax.random.normal(k4, (2 * DIM, LATENT_DIM), dtype=jnp.float32) * LATENT_DIM ** (-0.5)
        Wo = jax.random.normal(k5, (DIM, DIM), dtype=jnp.float32) * DIM ** (-0.5)
        return {'x': x, 'z': z, 'Wq': Wq, 'Wkv': Wkv, 'Wo': Wo}
    _L0_xattn_all = _L0_xattn_setup()
    _L0_xattn_in = {k: v for k, v in _L0_xattn_all.items() if k in ('Wq', 'Wkv', 'Wo')}
    del _L0_xattn_all

    def _L0_ffn_setup():
        import jax, jax.numpy as jnp
        import numpy as np
        TOP_K = 2
        key = jax.random.key(seed)
        k1, k2, k3, k4 = jax.random.split(key, 4)
        B, S, H, F, E = (2, 256, 128, 352, 8)
        hidden_states = jax.random.normal(k1, (B, S, H), dtype=jnp.float32)
        wqkv = jax.random.normal(k2, (3 * E, H), dtype=jnp.float32) * 0.02
        w1 = jax.random.normal(k3, (E, 2 * F, H), dtype=jnp.float32) * 0.02
        w2 = jax.random.normal(k4, (E, H, F), dtype=jnp.float32) * 0.02
        return {'hidden_states': hidden_states, 'wqkv': wqkv, 'w1': w1, 'w2': w2}
    _L0_ffn_all = _L0_ffn_setup()
    _L0_ffn_in = {k: v for k, v in _L0_ffn_all.items() if k in ('wqkv', 'w1', 'w2')}
    del _L0_ffn_all
    return {'x': x, 'ctx_512': ctx_512, 'g_xattn': g_xattn, 'g_ffn': g_ffn, 'L0_xattn_Wq': _L0_xattn_in['Wq'], 'L0_xattn_Wkv': _L0_xattn_in['Wkv'], 'L0_xattn_Wo': _L0_xattn_in['Wo'], 'L0_ffn_wqkv': _L0_ffn_in['wqkv'], 'L0_ffn_w1': _L0_ffn_in['w1'], 'L0_ffn_w2': _L0_ffn_in['w2']}

def reference(x, ctx_512, g_xattn, g_ffn, L0_xattn_Wq, L0_xattn_Wkv, L0_xattn_Wo, L0_ffn_wqkv, L0_ffn_w1, L0_ffn_w2):
    import jax
    import jax.numpy as jnp

    def _L0_xattn_ref(x, z, Wq, Wkv, Wo):
        import jax, jax.numpy as jnp
        import numpy as np
        DIM = 128
        LATENT_DIM = 64
        NUM_HEADS = 16
        HEAD_DIM = DIM // NUM_HEADS
        SCALE = HEAD_DIM ** (-0.5)
        B, xN, _ = x.shape
        _, zN, _ = z.shape
        Q = (x @ Wq.T).reshape(B, xN, NUM_HEADS, HEAD_DIM)
        KV = (z @ Wkv.T).reshape(B, zN, 2, NUM_HEADS, HEAD_DIM)
        K = KV[:, :, 0]
        V = KV[:, :, 1]
        attn = jnp.einsum('bqhd,bkhd->bhqk', Q, K) * SCALE
        attn = jax.nn.softmax(attn, axis=-1)
        O = jnp.einsum('bhqk,bkhd->bqhd', attn, V).reshape(B, xN, DIM)
        return O @ Wo.T

    def _L0_ffn_ref(hidden_states, wqkv, w1, w2):
        import jax, jax.numpy as jnp
        import numpy as np
        TOP_K = 2
        b, s, h = hidden_states.shape
        E = w1.shape[0]
        mixed = hidden_states @ wqkv.T
        q, k, v = jnp.split(mixed, 3, axis=-1)
        q = q.astype(jnp.float32)
        k = k.astype(jnp.float32)
        v = v.astype(jnp.float32)
        attn = jax.nn.softmax(q[..., :, None] * k[..., None, :], axis=-1)
        logits = jnp.einsum('bsej,bsj->bse', attn, v).reshape(-1, E)
        top_logits, idx = jax.lax.top_k(logits, TOP_K)
        scores = jax.nn.softmax(top_logits.astype(jnp.float32), axis=-1).astype(hidden_states.dtype)
        N = b * s
        x = hidden_states.reshape(N, h)
        token_ids = jnp.repeat(jnp.arange(N), TOP_K)
        expert_ids = idx.reshape(-1)
        x_rep = x[token_ids]
        out = jnp.zeros_like(x_rep)
        for e in range(E):
            h1 = x_rep @ w1[e].T
            a, g = jnp.split(h1, 2, axis=-1)
            he = jax.nn.silu(a) * g @ w2[e].T
            out = out + jnp.where((expert_ids == e)[:, None], he, jnp.zeros((), out.dtype))
        out = out * scores.reshape(-1, 1)
        combined = out.reshape(N, TOP_K, h).sum(axis=1)
        return combined.reshape(b, s, h)
    x = x + jnp.tanh(g_xattn[0]) * _L0_xattn_ref(_layernorm(x, axis=-1), ctx_512, L0_xattn_Wq, L0_xattn_Wkv, L0_xattn_Wo)
    x = x + jnp.tanh(g_ffn[0]) * _L0_ffn_ref(_layernorm(x, axis=-1), L0_ffn_wqkv, L0_ffn_w1, L0_ffn_w2)
    return x

_drawn_inputs = setup_inputs


def setup_inputs(seed=0):
    import zlib

    import numpy as np

    out = dict(_drawn_inputs(seed))
    spreads = {}
    factors = {'L0_ffn_wqkv': 8.0, 'L0_ffn_w1': 8.0, 'L0_ffn_w2': 8.0}
    for name, (base, spread) in spreads.items():
        noise = np.random.default_rng([zlib.crc32(name.encode()), seed]).standard_normal(out[name].shape)
        drawn = base * np.exp(spread * noise) if base else spread * noise
        out[name] = jnp.asarray(drawn.astype(out[name].dtype))
    for name, factor in factors.items():
        out[name] = (out[name] * factor).astype(out[name].dtype)
    return out
```

```python
from contextlib import ExitStack

import numpy as np

import concourse.bass as bass
from concourse import mybir

F32 = mybir.dt.float32
BF16 = mybir.dt.bfloat16
ALU = mybir.AluOpType
ACT = mybir.ActivationFunctionType
AX = mybir.AxisListType

B, NQ, D = 32, 100, 128
NK, L = 1444, 64
H, HD = 16, 8
NP = H // 2
E, F = 8, 352
EPS = 1e-5
SCALE = HD ** -0.5
LOWEST = -3.0e38

KT = -(-NK // 128)
ROWS = H * NQ
RT = -(-ROWS // 128)
CH = [482, 482, 480]
CO = [0, 482, 964]
NC = len(CH)
SM = RT * NC
UNITS = 2 * KT
HW = ROWS // 2
PW = 2 * NQ
KPART = [0, 0, 0, 1, 1, 2]
QPART = [0, 1, 2, 0, 1, 0]
UROWS = len(KPART) * HD
KROWS = 2 * UROWS + 2
CB = 4
CT = CB * NQ
NCH = B // CB
FT = [(0, 128), (128, 128), (256, 96)]
DMA = 16
COPIES = 2 * len(KPART)

AHEAD = 13
PLAN = [[] for _ in range(UNITS)]
for _u, _use in ((3, ("v", 1, 0)), (5, ("v", 1, 1)), (6, ("v", 1, 2)), (7, ("o", -1, 0)), (9, ("k", 2, 0)),
                 (10, ("k", 2, 1)), (11, ("y", -1, 0)), (12, ("k", 2, 2)), (17, ("m", 1, 0))):
    PLAN[_u].append(_use)
_n = AHEAD
for _u in range(UNITS):
    _take = range(_n, _n + 2 - len(PLAN[_u]))
    PLAN[_u] = [("s", 1, m) if m < SM else ("t", 2, m - SM) for m in _take] + PLAN[_u]
    _n = _take.stop
assert _n == SM + AHEAD
FIRST = [("k", 0, n) for n in range(NC)] + [("s", 0, n) for n in range(SM)] + [("k", 1, n) for n in range(NC)] \
    + [("m", 0, 0)] + [("s", 1, n) for n in range(4)] + [("v", 0, n) for n in range(NC)] \
    + [("s", 1, n) for n in range(4, AHEAD)]
ALL = "skvmoyt"


def kinds_of(i):
    return "skvmt" if i == 0 else "svmoy" if i == B - 2 else "oy" if i == B - 1 else ALL


def uses_of(kinds):
    return [use for units in PLAN for use in units if use[0] in kinds]


def key_rows(t):
    return min(128, NK - 128 * t)


def score_rows(t):
    return min(128, ROWS - 128 * t)


def build(nc, x, ctx_t, g_x, g_f, wq_t, wk_t, wv_t, wo_t, wr_t, w1_t, w2_t,
          ident, head_mask, pick_num, pick_den, rank, out):
    with ExitStack() as stack:
        def sb(name, shape, dt=F32):
            return stack.enter_context(nc.sbuf_tensor(name, shape, dt))

        def sem(name):
            return stack.enter_context(nc.semaphore(name))

        xs = sb("xs", [NQ, B * D])
        q_part = sb("q_part", [128, 3, B * NQ], BF16)
        ctx = sb("ctx", [L, 2, NK])
        k_full = sb("k_full", [128, NK])
        k_rest = sb("k_rest", [128, NK])
        k_hi = sb("k_hi", [128, 2, NK], BF16)
        k_mid = sb("k_mid", [128, NK], BF16)
        k_lo = sb("k_lo", [128, NK], BF16)
        k_stack = sb("k_stack", [128, 2, NP, NK], BF16)
        q_full = sb("q_full", [128, 2, CT])
        q_rest = sb("q_rest", [128, 2, CT])
        q_stack = sb("q_stack", [KROWS, 2, RT * 128], BF16)
        v_ones = sb("v_ones", [128, 2, KT, NP, 32])
        probs = sb("probs", [128, 4, HW])
        q_block = sb("q_block", [128, 2, H, NQ], BF16)
        maxes = sb("maxes", [128, RT, NC])
        neg_max = sb("neg_max", [128, RT])
        max_row = sb("max_row", [RT, 2, 128], BF16)
        o_sum = sb("o_sum", [128, 4 * NQ])
        den_inv = sb("den_inv", [128, NQ])
        o_norm = sb("o_norm", [128, NQ])
        xn = sb("xn", [NQ, 2, CT * D // NQ])
        wq = sb("wq", [D, D])
        wk = sb("wk", [L, D])
        wv = sb("wv", [L, D])
        wo = sb("wo", [D, D])
        wr = sb("wr", [D, 3 * E])
        idn = sb("idn", [128, 128])
        hmask = sb("hmask", [128, H], BF16)
        pnum = sb("pnum", [128, 4, 128])
        pden = sb("pden", [128, 4, 128])
        rnk = sb("rnk", [NQ, E])
        g_in = sb("g_in", [NQ, 2])
        g_tanh = sb("g_tanh", [NQ, 2])
        stats = sb("stats", [NQ, B * 6])
        mean = sb("mean", [NQ, B])
        rstd = sb("rstd", [NQ, B])
        tmp = sb("tmp", [NQ, 4, B])
        mixed = sb("mixed", [NQ, B, 3 * E])
        route = sb("route", [NQ, 8, B, E])
        pick = sb("pick", [NQ, 6, B])
        gates = sb("gates", [NQ, B * E])

        xt = probs[:].rearrange("p a b -> p (a b)")
        k_flat = k_stack[:].rearrange("p a b n -> p (a b n)").bitcast(F32)
        w1 = k_flat[:, 0:E * 2 * F]
        w2 = k_flat[:, E * 2 * F:E * (2 * F + len(FT) * D)].rearrange("p (e t d) -> p e t d", e=E, t=len(FT))
        v_flat = v_ones[:].rearrange("p a b c d -> p (a b c d)")
        outer = [v_flat[0:NQ, n * B * E * E:(n + 1) * B * E * E].rearrange("q (b i j) -> q b i j", b=B, i=E)
                 for n in range(3)]
        q_flat = q_part[:].rearrange("p a n -> p (a n)").bitcast(F32)
        silu = q_flat[:, 0:3 * CT].rearrange("p (t n) -> p t n", t=3)
        hid = q_flat[:, 3 * CT:9 * CT].rearrange("p (a t n) -> p a t n", a=2, t=3)

        ps = stack.enter_context(nc.psum_tensor("ps", [128, 8, 512], F32))
        RING, OB = 4, 7

        x_in = sem("x_in")
        const_in = sem("const_in")
        w_in = sem("w_in")
        ctx_in = [sem("ctx_in0"), sem("ctx_in1")]
        k_in = sem("k_in")
        q_in = sem("q_in")
        max_in = sem("max_in")
        cleared = sem("cleared")
        v_step = sem("v_step")
        a_step = sem("a_step")
        v_asks = sem("v_asks")
        tanh_done = sem("tanh_done")
        stats_ready = sem("stats_ready")
        xn_ready = sem("xn_ready")
        xn_turned = sem("xn_turned")
        xt_ready = sem("xt_ready")
        q_made = sem("q_made")
        q_scaled = sem("q_scaled")
        q_split = sem("q_split")
        k_made = sem("k_made")
        k_taken = sem("k_taken")
        k_parted = sem("k_parted")
        v_made = sem("v_made")
        v_taken = sem("v_taken")
        block_ready = sem("block_ready")
        sm_made = sem("sm_made")
        sm_taken = sem("sm_taken")
        neg_ready = sem("neg_ready")
        max_turned = sem("max_turned")
        row_ready = sem("row_ready")
        st_made = sem("st_made")
        exp_done = sem("exp_done")
        pv_done = sem("pv_done")
        o_copied = sem("o_copied")
        nd_made = sem("nd_made")
        inv_ready = sem("inv_ready")
        on_ready = sem("on_ready")
        y_made = sem("y_made")
        y_added = sem("y_added")
        mixed_made = sem("mixed_made")
        mixed_taken = sem("mixed_taken")
        h_made = sem("h_made")
        silu_done = sem("silu_done")
        h_ready = sem("h_ready")
        e_made = sem("e_made")
        e_added = sem("e_added")
        out_done = sem("out_done")

        block = stack.enter_context(nc.Block())

        def at(i, it, off):
            return i + off

        def ring_read(eng, kind, b, n):
            if kind in "st":
                eng.wait_ge(sm_taken, b * SM + n + 1)
            elif kind == "k":
                eng.wait_ge(k_taken, b * NC + n + 1)
            elif kind == "v":
                eng.wait_ge(v_taken, b * NC + n + 1)
            elif kind == "m":
                eng.wait_ge(row_ready, b * 2 + 2)
            elif kind == "o":
                eng.wait_ge(on_ready, b + 1)
            else:
                eng.wait_ge(y_added, b + 1)

        def batches(eng, body, last=B):
            for i in (0, 1):
                body(i, 0, i, kinds_of(i), kinds_of(i - 1) if i else None)
            with eng.Fori(1, B // 2 - 1) as it:
                for par in (0, 1):
                    body(it * 2 + par, it, par, ALL, ALL)
            for i in (B - 2, B - 1):
                body(i, i // 2, i % 2, kinds_of(i), kinds_of(i - 1))

        @block.sync
        def _(sp):
            step = CB * 2
            for dst, src in ((idn, ident), (wq, wq_t), (wk, wk_t)):
                sp.dma_start(dst[:], src).then_inc(const_in, DMA)
            sp.dma_start(ctx[:, 0, :], ctx_t[0]).then_inc(ctx_in[0], DMA)
            for n in range(0, B, step):
                sp.dma_start(xs[:, n * D:(n + step) * D].rearrange("q (b d) -> q b d", b=step),
                             x[n:n + step].rearrange("b q d -> q b d")).then_inc(x_in, DMA)
            sp.dma_start(ctx[:, 1, :], ctx_t[1]).then_inc(ctx_in[1], DMA)
            for dst, src in ((hmask, head_mask), (wv, wv_t), (wo, wo_t), (wr, wr_t), (rnk, rank),
                             (pnum, pick_num), (pden, pick_den)):
                sp.dma_start(dst[:], src).then_inc(const_in, DMA)
            for n, g in enumerate((g_x, g_f)):
                sp.dma_start(g_in[:, n:n + 1], g.rearrange("(a b) -> a b", a=1).to_broadcast([NQ, 1])) \
                    .then_inc(const_in, DMA)

            def held(value):
                return value if isinstance(value, int) else sp.snap(sp.to_reg(value))

            def stacks(b, par, parts, tokens):
                sp.wait_ge(k_taken, parts)
                sp.wait_ge(k_parted, parts)
                for s, part in enumerate(KPART):
                    src = (k_hi[:, par, :], k_mid[:], k_lo[:])[part]
                    for u in (0, 1):
                        r = u * UROWS + s * HD
                        sp.dma_start(k_stack[r:r + HD, par, :, :], src[64 * u:64 * u + 64, :]).then_inc(k_in, DMA)
                if isinstance(b, int) and b == 0:
                    sp.wait_ge(q_split, 1)
                for s, part in enumerate(QPART):
                    for u in (0, 1):
                        r = u * UROWS + s * HD
                        dst = q_stack[r:r + HD, par, 0:ROWS].rearrange("p (h n) -> p h n", h=NP)
                        sp.dma_start(dst[:, :, u * NQ:(u + 1) * NQ],
                                     q_part[64 * u:64 * u + 64, part, bass.ds(tokens, NQ)]).then_inc(q_in, DMA)

            def max_rows(par, parts):
                sp.wait_ge(row_ready, parts)
                for n in (0, 1):
                    dst = q_stack[2 * UROWS + n:2 * UROWS + n + 1, par, :].rearrange("p (t n) -> p t n", t=RT)
                    sp.dma_start(dst, max_row[:, n, :]).then_inc(max_in, DMA)

            sp.wait_ge(cleared, 6)
            stacks(0, 0, NC, 0)
            sp.wait_ge(v_made, NC)
            max_rows(0, 2)
            sp.wait_ge(q_split, NCH)

            def body(i, it, par, kinds, before):
                if "s" not in kinds:
                    return
                units, copies, copied = held(i * UNITS), held((i + 1) * (COPIES * DMA)), held((i + 1) * (2 * DMA))
                parts, tokens, turned = held((i + 2) * NC), held((i + 1) * NQ), held((i + 2) * 2)
                if "k" in kinds:
                    src = ctx_t[bass.ds(i + 2, 1)].rearrange("a l k -> (a l) k")
                    sp.dma_start(ctx[:, par, :], src).then_inc(ctx_in[par], DMA)
                if "o" in kinds:
                    sp.wait_ge(st_made, units)
                sp.wait_ge(k_in, copies)
                sp.wait_ge(q_in, copies)
                stacks(i + 1, 1 - par, parts, tokens)
                sp.wait_ge(max_in, copied)
                sp.wait_ge(v_made, parts)
                max_rows(1 - par, turned)

            batches(sp, body)
            sp.wait_ge(st_made, B * UNITS)
            sp.dma_start(w1, w1_t).then_inc(w_in, DMA)
            for t, (f0, fr) in enumerate(FT):
                sp.dma_start(w2[0:fr, :, t, :], w2_t[:, f0:f0 + fr, :].rearrange("e f d -> f e d")).then_inc(w_in, DMA)
            with sp.Fori(0, NCH) as c:
                sp.wait_ge(e_added, c * E + E)
                sp.dma_start(out[bass.ds(c * CB, CB)].rearrange("b q d -> q b d"),
                             xs[:, bass.ds(c * (CB * D), CB * D)].rearrange("q (b d) -> q b d", b=CB)) \
                    .then_inc(out_done, DMA)
            sp.wait_ge(out_done, NCH * DMA)

        @block.gpsimd
        def _(pool):
            pool.memset(q_stack[:], 0.0).then_inc(cleared, 1)
            pool.memset(maxes[:], 0.0).then_inc(cleared, 1)
            pool.memset(v_ones[:, :, :, :, 2 * HD:32], 1.0).then_inc(cleared, 1)
            pool.wait_ge(cleared, 3)
            pool.memset(v_ones[:, :, KT - 1, :, :], 0.0).then_inc(cleared, 1)
            pool.wait_ge(cleared, 4)
            pool.memset(v_ones[0:key_rows(KT - 1), :, KT - 1, :, 2 * HD:32], 1.0).then_inc(cleared, 1)
            pool.memset(k_stack[2 * UROWS:KROWS, :, :, :], 1.0).then_inc(cleared, 1)

            def block_q(b, par):
                q = q_part[:, 0, bass.ds(b * NQ, NQ)]
                pool.tensor_tensor(q_block[:, par, :, :], q.unsqueeze(1).to_broadcast([128, H, NQ]),
                                   hmask[:].unsqueeze(2).to_broadcast([128, H, NQ]), ALU.mult).then_inc(block_ready, 1)

            def part_k(b, par):
                pool.wait_ge(k_taken, (b + 1) * NC)
                if not (isinstance(b, int) and b == 0):
                    pool.wait_ge(k_in, b * COPIES * DMA)
                pool.tensor_tensor(k_mid[:], k_full[:], k_hi[:, par, :], ALU.subtract).then_inc(k_parted, 1)
                pool.tensor_tensor(k_rest[:], k_full[:], k_hi[:, par, :], ALU.subtract).then_inc(k_parted, 1)
                pool.wait_ge(k_parted, b * 3 + 2)
                pool.tensor_tensor(k_lo[:], k_rest[:], k_mid[:], ALU.subtract).then_inc(k_parted, 1)

            pool.wait_ge(const_in, DMA * 12)
            part_k(0, 0)
            pool.wait_ge(q_scaled, 1)
            block_q(0, 0)
            block_q(1, 1)
            part_k(1, 1)
            pool.wait_ge(q_scaled, NCH)

            def body(i, it, par, kinds, before):
                if "k" in kinds:
                    pool.wait_ge(sm_made, (i + 1) * SM)
                    block_q(i + 2, par)
                    part_k(i + 2, par)

            batches(pool, body)

        @block.scalar
        def _(act):
            act.wait_ge(const_in, DMA * 12)
            act.wait_ge(cleared, 6)
            act.activation(g_tanh[:], g_in[:], ACT.Tanh).then_inc(tanh_done, 1)

            def root(phase):
                act.wait_ge(v_asks, 1 if phase == 0 else 2)
                act.activation(tmp[:, 3, :], tmp[:, 2, :], ACT.Sqrt).then_inc(a_step, 1)

            def take_xt(phase, c):
                act.wait_ge(xn_turned, phase * NCH + c + 1)
                act.activation(xt[:, c * CT:(c + 1) * CT], ps[:, c % 2, 0:CT], ACT.Copy).then_inc(xt_ready, 1)

            def take_first(uses):
                for n_use, (kind, b, n) in enumerate(uses):
                    if kind == "k":
                        take_k(b, 0, b % 2, n, RING + n_use % 3)
                    elif kind == "v":
                        take_v(b, b % 2, n, RING + n_use % 3)

            def take_q(c):
                if c >= 2:
                    act.wait_ge(q_split, c - 1)
                act.wait_ge(q_made, c + 1)
                src = ps[:, 2 + c % 2, 0:CT]
                act.activation(q_full[:, c % 2, :], src, ACT.Copy, scale=SCALE)
                act.activation(q_part[:, 0, c * CT:(c + 1) * CT], src, ACT.Copy, scale=SCALE).then_inc(q_scaled, 1)

            def take_k(b, it, par, n, bank):
                act.wait_ge(k_made, b * NC + n + 1)
                if n == 0 and not isinstance(b, int) or n == 0 and b >= 1:
                    act.wait_ge(k_parted, b * 3)
                if n == 0 and (not isinstance(b, int) or b >= 2):
                    act.wait_ge(sm_made, (b - 1) * SM)
                    act.wait_ge(k_in, (b - 1) * COPIES * DMA)
                src = ps[:, bank, 0:CH[n]]
                act.activation(k_full[:, CO[n]:CO[n] + CH[n]], src, ACT.Copy)
                act.activation(k_hi[:, par, CO[n]:CO[n] + CH[n]], src, ACT.Copy).then_inc(k_taken, 1)

            def take_v(b, par, n, bank):
                act.wait_ge(v_made, b * NC + n + 1)
                if n == 0 and (not isinstance(b, int) or b >= 2):
                    act.wait_ge(pv_done, (b - 1) * UNITS)
                full = sum(key_rows(t) == 128 for t in range(4 * n, 4 * n + 4))
                src = ps[:, bank, :].rearrange("p (t h c) -> p t h c", t=4, h=NP)
                dst = v_ones[:, par, 4 * n:4 * n + 4, :, 0:2 * HD]
                last = act.activation(dst[:, 0:full], src[:, 0:full], ACT.Copy)
                if full < 4:
                    r = key_rows(KT - 1)
                    last = act.activation(dst[0:r, full], src[0:r, full], ACT.Copy)
                last.then_inc(v_taken, 1)

            take_first(FIRST[:NC])
            root(0)
            for c in range(NCH):
                take_xt(0, c)
                if c >= 1:
                    take_q(c - 1)
            take_q(NCH - 1)
            take_first([("", 0, 0)] * NC + FIRST[NC:])
            used = [len(FIRST)]

            def copy_o(b, last=False):
                act.wait_ge(pv_done, (b + 1) * UNITS)
                if not isinstance(b, int) or b >= 1:
                    act.wait_ge(nd_made, b)
                act.activation(o_sum[:], ps[:, OB, 0:4 * NQ], ACT.Copy).then_inc(o_copied, 1)

            def body(i, it, par, kinds, before):
                for u in range(UNITS):
                    act.wait_ge(st_made, i * UNITS + u + 1)
                    if not isinstance(i, int) or i * UNITS + u >= 4:
                        act.wait_ge(pv_done, i * UNITS + u - 3)
                    r = key_rows(u // 2)
                    act.activation(probs[0:r, u % 4, :].rearrange("p (a n) -> p a n", a=2),
                                   ps[0:r, 2 * (u % 2):2 * (u % 2) + 2, 0:CT], ACT.Exp).then_inc(exp_done, 1)
                    if u == 1 and "o" in kinds:
                        copy_o(i - 1)
                    for kind, off, n in PLAN[u]:
                        if kind in kinds:
                            bank = RING + used[0] % 3
                            used[0] += 1
                            if kind == "k":
                                take_k(i + off, it, par, n, bank)
                            elif kind == "v":
                                take_v(i + off, 1 - par, n, bank)

            batches(act, body)
            copy_o(B - 1)
            root(1)
            for c in range(NCH):
                take_xt(1, c)
            for g in range(2):
                act.wait_ge(mixed_made, g + 1)
                act.activation(mixed[:, g * B // 2:(g + 1) * B // 2, :],
                               ps[0:NQ, 2 + g, 0:B // 2 * 3 * E].rearrange("q (b e) -> q b e", b=B // 2),
                               ACT.Copy).then_inc(mixed_taken, 1)
            act.wait_ge(v_asks, 3)
            act.activation(outer[1], outer[0], ACT.Exp).then_inc(a_step, 1)
            act.wait_ge(v_asks, 4)
            act.activation(pick[:, 3, :], pick[:, 2, :], ACT.Exp).then_inc(a_step, 1)

            def silus(c, e, first):
                for t, (f0, fr) in enumerate(FT):
                    n = (c * E + e) * len(FT) + t
                    act.wait_ge(h_made, n + 1)
                    if not (first and e == 0):
                        act.wait_ge(h_ready, n - 2)
                    act.activation(silu[0:fr, t, :], ps[0:fr, 2 * t, 0:CT], ACT.Silu).then_inc(silu_done, 1)

            for e in range(E):
                silus(0, e, True)
            with act.Fori(1, NCH) as c:
                for e in range(E):
                    silus(c, e, False)

        @block.vector
        def _(dve):
            steps = [0]

            def step(ins):
                ins.then_inc(v_step, 1)
                steps[0] += 1
                dve.wait_ge(v_step, steps[0])

            def norm(phase):
                dve.wait_ge(stats_ready, (phase + 1) * B)
                st = stats[:].rearrange("q (b s) -> q s b", s=6)
                step(dve.tensor_tensor(tmp[:, 0, :], st[:, 1, :], st[:, 4, :], ALU.add))
                step(dve.tensor_scalar(mean[:], tmp[:, 0, :], 0.5, None, ALU.mult))
                step(dve.tensor_tensor(tmp[:, 1, :], st[:, 1, :], st[:, 4, :], ALU.subtract))
                step(dve.tensor_tensor(tmp[:, 0, :], tmp[:, 1, :], tmp[:, 1, :], ALU.mult))
                step(dve.scalar_tensor_tensor(tmp[:, 1, :], tmp[:, 0, :], D / 4, st[:, 2, :], ALU.mult, ALU.add))
                step(dve.tensor_tensor(tmp[:, 0, :], tmp[:, 1, :], st[:, 5, :], ALU.add))
                dve.tensor_scalar(tmp[:, 2, :], tmp[:, 0, :], 1.0 / D, EPS, ALU.mult, ALU.add).then_inc(v_asks, 1)
                dve.wait_ge(a_step, 1 if phase == 0 else 2)
                step(dve.reciprocal(tmp[:, 0, :], tmp[:, 3, :]))
                step(dve.tensor_tensor(tmp[:, 1, :], tmp[:, 0, :], tmp[:, 0, :], ALU.mult))
                step(dve.tensor_tensor(tmp[:, 3, :], tmp[:, 1, :], tmp[:, 2, :], ALU.mult))
                step(dve.tensor_scalar(tmp[:, 1, :], tmp[:, 3, :], -0.5, 1.5, ALU.mult, ALU.add))
                step(dve.tensor_tensor(rstd[:], tmp[:, 0, :], tmp[:, 1, :], ALU.mult))

            def norm_chunk(phase, c):
                n = phase * NCH + c
                if n >= 2:
                    dve.wait_ge(xn_turned, n - 1)
                for t in range(CB):
                    b = c * CB + t
                    ins = dve.tensor_scalar(xn[:, c % 2, t * D:(t + 1) * D], xs[:, b * D:(b + 1) * D],
                                            mean[:, b:b + 1], rstd[:, b:b + 1], ALU.subtract, ALU.mult)
                ins.then_inc(xn_ready, 1)

            def split_q(c):
                of = slice(c * CT, (c + 1) * CT)
                dve.wait_ge(q_scaled, c + 1)
                full, rest = q_full[:, c % 2, :], q_rest[:, c % 2, :]
                step(dve.tensor_tensor(rest, full, q_part[:, 0, of], ALU.subtract))
                step(dve.tensor_copy(q_part[:, 1, of], rest))
                dve.tensor_tensor(q_part[:, 2, of], rest, q_part[:, 1, of], ALU.subtract).then_inc(q_split, 1)

            def statistics(b):
                dve.bn_stats(stats[:, bass.ds(b * 6, 6)], xs[:, bass.ds(b * D, D)]).then_inc(stats_ready, 1)

            dve.wait_ge(x_in, (B // CB // 2) * DMA)
            with dve.Fori(0, B) as b:
                statistics(b)
            norm(0)
            for c in range(NCH):
                norm_chunk(0, c)
                if c >= 1:
                    split_q(c - 1)
            split_q(NCH - 1)

            def take_max(b, n, bank):
                t, c = n // NC, n % NC
                r = score_rows(t)
                dve.wait_ge(sm_made, b * SM + n + 1)
                if n == 0 and (not isinstance(b, int) or b >= 1):
                    dve.wait_ge(neg_ready, b)
                dve.tensor_reduce(maxes[0:r, t, c:c + 1], ps[0:r, bank, 0:CH[c]], AX.X, ALU.max).then_inc(sm_taken, 1)
                if n == SM - 1:
                    dve.wait_ge(sm_taken, b * SM + SM)
                    dve.tensor_reduce(neg_max[:], maxes[:], AX.X, ALU.max, negate=True).then_inc(neg_ready, 1)

            def part_max(b, bank):
                dve.wait_ge(max_turned, b + 1)
                if not isinstance(b, int) or b >= 1:
                    dve.wait_ge(max_in, b * 2 * DMA)
                dve.tensor_copy(max_row[:, 0, :], ps[0:RT, bank, 0:128]).then_inc(row_ready, 1)
                dve.wait_ge(row_ready, b * 2 + 1)
                dve.tensor_tensor(max_row[:, 1, :], ps[0:RT, bank, 0:128], max_row[:, 0, :], ALU.subtract) \
                    .then_inc(row_ready, 1)

            def divide(b, bank):
                dve.wait_ge(nd_made, b + 1)
                dve.reciprocal(den_inv[:], ps[:, bank, 0:NQ]).then_inc(inv_ready, 1)
                dve.wait_ge(inv_ready, b + 1)
                if not isinstance(b, int) or b >= 1:
                    dve.wait_ge(y_made, b)
                dve.tensor_tensor(o_norm[:], ps[:, bank, 128:128 + NQ], den_inv[:], ALU.mult).then_inc(on_ready, 1)

            def add_y(b, bank):
                dve.wait_ge(y_made, b + 1)
                row = xs[:, bass.ds(b * D, D)]
                dve.scalar_tensor_tensor(row, ps[0:NQ, bank, 0:D], g_tanh[:, 0:1], row, ALU.mult, ALU.add) \
                    .then_inc(y_added, 1)
                dve.wait_ge(y_added, b + 1)
                statistics(b)

            dve.wait_ge(cleared, 6)
            dve.wait_ge(tanh_done, 1)
            used = [0]

            def take(kind, b, n):
                bank = RING + used[0] % 3
                used[0] += 1
                if kind in "st":
                    take_max(b, n, bank)
                elif kind == "m":
                    part_max(b, bank)
                elif kind == "o":
                    divide(b, bank)
                elif kind == "y":
                    add_y(b, bank)

            for kind, b, n in FIRST:
                take(kind, b, n)

            def body(i, it, par, kinds, before):
                for kind, off, n in uses_of(kinds):
                    take(kind, i + off, n)

            batches(dve, body)
            take("o", B - 1, 0)
            take("y", B - 1, 0)

            norm(1)
            for c in range(NCH):
                norm_chunk(1, c)
            dve.wait_ge(mixed_taken, 2)
            q, k, v = (mixed[:, :, n * E:(n + 1) * E] for n in range(3))
            wide = [NQ, B, E, E]
            step(dve.tensor_tensor(outer[2], q.unsqueeze(3).to_broadcast(wide), k.unsqueeze(2).to_broadcast(wide),
                                   ALU.mult))
            step(dve.tensor_reduce(route[:, 0, :, :], outer[2], AX.X, ALU.max))
            dve.tensor_tensor(outer[0], outer[2], route[:, 0, :, :].unsqueeze(3).to_broadcast(wide), ALU.subtract) \
                .then_inc(v_asks, 1)
            dve.wait_ge(a_step, 3)
            step(dve.tensor_reduce(route[:, 1, :, :], outer[1], AX.X, ALU.add))
            step(dve.tensor_tensor(outer[2], outer[1], v.unsqueeze(2).to_broadcast(wide), ALU.mult))
            step(dve.tensor_reduce(route[:, 2, :, :], outer[2], AX.X, ALU.add))
            step(dve.reciprocal(route[:, 3, :, :], route[:, 1, :, :]))
            logits = route[:, 0, :, :]
            step(dve.tensor_tensor(logits, route[:, 2, :, :], route[:, 3, :, :], ALU.mult))

            def over_e(t):
                return t.unsqueeze(2).to_broadcast([NQ, B, E])

            def best(values, chosen, top):
                step(dve.tensor_reduce(top, values, AX.X, ALU.max))
                step(dve.tensor_tensor(route[:, 4, :, :], values, over_e(top), ALU.is_equal))
                step(dve.tensor_tensor(route[:, 5, :, :], route[:, 4, :, :],
                                       rnk[:].unsqueeze(1).to_broadcast([NQ, B, E]), ALU.mult))
                step(dve.tensor_reduce(pick[:, 4, :], route[:, 5, :, :], AX.X, ALU.max))
                step(dve.tensor_tensor(chosen, route[:, 5, :, :], over_e(pick[:, 4, :]), ALU.is_equal))

            best(logits, route[:, 1, :, :], pick[:, 0, :])
            step(dve.scalar_tensor_tensor(route[:, 3, :, :], route[:, 1, :, :], LOWEST, logits, ALU.mult, ALU.add))
            best(route[:, 3, :, :], route[:, 2, :, :], pick[:, 1, :])
            dve.tensor_tensor(pick[:, 2, :], pick[:, 1, :], pick[:, 0, :], ALU.subtract).then_inc(v_asks, 1)
            dve.wait_ge(a_step, 4)
            step(dve.tensor_scalar(pick[:, 4, :], pick[:, 3, :], 1.0, None, ALU.add))
            step(dve.reciprocal(pick[:, 5, :], pick[:, 4, :]))
            step(dve.tensor_scalar(pick[:, 4, :], pick[:, 5, :], g_tanh[:, 1:2], None, ALU.mult))
            step(dve.tensor_tensor(pick[:, 5, :], pick[:, 4, :], pick[:, 3, :], ALU.mult))
            step(dve.tensor_tensor(route[:, 4, :, :], route[:, 1, :, :], over_e(pick[:, 4, :]), ALU.mult))
            step(dve.tensor_tensor(route[:, 5, :, :], route[:, 2, :, :], over_e(pick[:, 5, :]), ALU.mult))
            step(dve.tensor_tensor(gates[:].rearrange("q (b e) -> q b e", b=B), route[:, 4, :, :],
                                   route[:, 5, :, :], ALU.add))

            def gate_h(c, e, first):
                for t, (f0, fr) in enumerate(FT):
                    s = c * E + e
                    dve.wait_ge(silu_done, s * len(FT) + t + 1)
                    if t == 0 and not (first and e < 2):
                        dve.wait_ge(e_made, s - 1)
                    dve.tensor_tensor(hid[0:fr, e % 2, t, :], silu[0:fr, t, :], ps[0:fr, 2 * t + 1, 0:CT], ALU.mult) \
                        .then_inc(h_ready, 1)

            def add_expert(c, e, first):
                s = c * E + e
                dve.wait_ge(e_made, s + 1)
                if not (first and e == 0):
                    dve.wait_ge(e_added, s)
                for t in range(CB):
                    row = xs[:, bass.ds(c * (CB * D) + t * D, D)]
                    ins = dve.scalar_tensor_tensor(row, ps[0:NQ, 6 + e % 2, t * D:(t + 1) * D],
                                                   gates[:, bass.ds(c * (CB * E) + (t * E + e), 1)], row,
                                                   ALU.mult, ALU.add)
                ins.then_inc(e_added, 1)

            def experts(c, first):
                for e in range(E):
                    gate_h(c, e, first)
                    if e:
                        add_expert(c, e - 1, first)
                    elif not first:
                        add_expert(c - 1, E - 1, first)

            experts(0, True)
            with dve.Fori(1, NCH) as c:
                experts(c, False)
            add_expert(NCH - 1, E - 1, False)

        @block.tensor
        def _(pe):
            def turn_chunk(phase, c):
                pe.wait_ge(xn_ready, phase * NCH + c + 1)
                if phase or c >= 2:
                    pe.wait_ge(xt_ready, phase * NCH + c - 1)
                for t in range(CB):
                    mm = pe.transpose(ps[:, c % 2, t * NQ:(t + 1) * NQ], xn[:, c % 2, t * D:(t + 1) * D],
                                      idn[0:NQ, 0:NQ])
                mm.then_inc(xn_turned, 1)

            def make_q(c):
                pe.wait_ge(xt_ready, c + 1)
                if c >= 2:
                    pe.wait_ge(q_scaled, c - 1)
                pe.matmul(ps[:, 2 + c % 2, 0:CT], wq[:], xt[:, c * CT:(c + 1) * CT], start=True, stop=True) \
                    .then_inc(q_made, 1)

            def make_k(b, it, par, n, bank):
                if n == 0:
                    pe.wait_ge(ctx_in[par], (it + 1) * DMA)
                pe.matmul(ps[:, bank, 0:CH[n]], wk[:], ctx[:, par, CO[n]:CO[n] + CH[n]], start=True, stop=True) \
                    .then_inc(k_made, 1)

            def make_v(par, n, bank):
                for t in range(4 * n, 4 * n + 4):
                    r = key_rows(t)
                    mm = pe.matmul(ps[0:r, bank, (t % 4) * D:(t % 4 + 1) * D], ctx[:, par, t * 128:t * 128 + r],
                                   wv[:], start=True, stop=True)
                mm.then_inc(v_made, 1)

            def make_scores(b, par, n, bank):
                t, c = n // NC, n % NC
                r = score_rows(t)
                if t == 0:
                    pe.wait_ge(k_taken, b * NC + c + 1)
                if n == 0:
                    pe.wait_ge(block_ready, b + 1)
                rows = q_block[:, par, :, :].rearrange("p h n -> p (h n)")[:, t * 128:t * 128 + r]
                pe.matmul(ps[0:r, bank, 0:CH[c]], rows, k_hi[:, par, CO[c]:CO[c] + CH[c]],
                          start=True, stop=True).then_inc(sm_made, 1)

            def turn_max(b, bank):
                pe.wait_ge(neg_ready, b + 1)
                pe.transpose(ps[0:RT, bank, 0:128], neg_max[:], idn[:]).then_inc(max_turned, 1)

            def gather(b, bank):
                pe.wait_ge(o_copied, b + 1)
                for pick_, at_ in ((pden, 0), (pnum, 128)):
                    for n in range(4):
                        mm = pe.matmul(ps[:, bank, at_:at_ + NQ], pick_[:, n, :], o_sum[:, n * NQ:(n + 1) * NQ],
                                       start=(n == 0), stop=(n == 3))
                mm.then_inc(nd_made, 1)

            def make_y(b, bank):
                pe.wait_ge(on_ready, b + 1)
                pe.matmul(ps[0:NQ, bank, 0:D], o_norm[:], wo[:], start=True, stop=True).then_inc(y_made, 1)

            def make(kind, b, it, par, n, bank):
                if kind in "st":
                    make_scores(b, par, n, bank)
                elif kind == "k":
                    make_k(b, it, par, n, bank)
                elif kind == "v":
                    make_v(par, n, bank)
                elif kind == "m":
                    turn_max(b, bank)
                elif kind == "o":
                    gather(b, bank)
                else:
                    make_y(b, bank)

            used = [0]
            pe.wait_ge(const_in, DMA * 12)
            for n_use, (kind, b, n) in enumerate(FIRST):
                if n_use == NC:
                    for c in range(NCH):
                        turn_chunk(0, c)
                        if c >= 1:
                            make_q(c - 1)
                    make_q(NCH - 1)
                if n_use >= 3:
                    ring_read(pe, *FIRST[n_use - 3])
                make(kind, b, 0, b % 2, n, RING + n_use % 3)
            used[0] = len(FIRST)

            def scores(i, par, u):
                t, half = u // 2, u % 2
                r = key_rows(t)
                if u == 0:
                    pe.wait_ge(k_in, (i + 1) * COPIES * DMA)
                    pe.wait_ge(q_in, (i + 1) * COPIES * DMA)
                    pe.wait_ge(max_in, (i + 1) * 2 * DMA)
                if not isinstance(i, int) or i * UNITS + u >= 2:
                    pe.wait_ge(exp_done, i * UNITS + u - 1)
                for n in range(4):
                    hp = 4 * half + n
                    mm = pe.matmul(ps[0:r, 2 * (u % 2) + n // 2, (n % 2) * PW:(n % 2 + 1) * PW],
                                   k_stack[0:KROWS, par, hp, t * 128:t * 128 + r],
                                   q_stack[0:KROWS, par, hp * PW:(hp + 1) * PW], start=True, stop=True)
                mm.then_inc(st_made, 1)

            def product(i, par, u):
                t, half = u // 2, u % 2
                pe.wait_ge(exp_done, i * UNITS + u + 1)
                if u == 0:
                    pe.wait_ge(v_taken, (i + 1) * NC)
                    if not isinstance(i, int) or i >= 1:
                        pe.wait_ge(o_copied, i)
                for n in range(4):
                    mm = pe.matmul(ps[32 * n:32 * n + 32, OB, half * PW:(half + 1) * PW],
                                   v_ones[:, par, t, 4 * half + n, :], probs[:, u % 4, n * PW:(n + 1) * PW],
                                   start=(u == 0), stop=(t == KT - 1), skip_group_check=True)
                mm.then_inc(pv_done, 1)

            def body(i, it, par, kinds, before):
                uses = uses_of(kinds)
                past = [(k, o - 1, n) for k, o, n in uses_of(before)[-3:]] if before else \
                    [(k, o, n) for k, o, n in FIRST[-3:]]
                line = past + uses
                if len(line) < len(past) + 1:
                    line = past
                at_use = [3]
                for u in range(UNITS):
                    scores(i, par, u)
                    if u >= 2:
                        product(i, par, u - 2)
                    elif not isinstance(i, int) or i >= 1:
                        product(i - 1, 1 - par, UNITS - 2 + u)
                    for kind, off, n in PLAN[u]:
                        if kind in kinds:
                            k_, o_, n_ = line[at_use[0] - 3]
                            ring_read(pe, k_, i + o_, n_)
                            make(kind, i + off, it + 1, par if kind in "kt" else 1 - par, n, RING + used[0] % 3)
                            at_use[0] += 1
                            used[0] += 1

            batches(pe, body)
            for u in (UNITS - 2, UNITS - 1):
                product(B - 1, 1, u)
            ring_read(pe, "v", B - 1, NC - 1)
            gather(B - 1, RING + used[0] % 3)
            used[0] += 1
            make_y(B - 1, RING + used[0] % 3)

            def mix(c):
                pe.wait_ge(xt_ready, NCH + c + 1)
                for b in range(c * CB, (c + 1) * CB):
                    n = b % (B // 2)
                    mm = pe.matmul(ps[0:NQ, 2 + b // (B // 2), n * 3 * E:(n + 1) * 3 * E],
                                   xt[:, b * NQ:(b + 1) * NQ], wr[:], start=True, stop=True)
                if c % (NCH // 2) == NCH // 2 - 1:
                    mm.then_inc(mixed_made, 1)

            for c in range(NCH):
                turn_chunk(1, c)
                if c >= 1:
                    mix(c - 1)
            mix(NCH - 1)

            pe.wait_ge(w_in, (1 + len(FT)) * DMA)
            pe.wait_ge(mixed_taken, 2)
            pe.wait_ge(y_added, B)

            def first_product(c, e, first):
                for t, (f0, fr) in enumerate(FT):
                    n = (c * E + e) * len(FT) + t
                    if not (first and e == 0):
                        pe.wait_ge(h_ready, n - 2)
                    for half in (0, 1):
                        at_ = e * 2 * F + half * F + f0
                        mm = pe.matmul(ps[0:fr, 2 * t + half, 0:CT], w1[:, at_:at_ + fr],
                                       xt[:, bass.ds(c * CT, CT)], start=True, stop=True)
                    mm.then_inc(h_made, 1)

            def second_product(c, e, first):
                s = c * E + e
                pe.wait_ge(h_ready, (s + 1) * len(FT))
                if not (first and e < 2):
                    pe.wait_ge(e_added, s - 1)
                for m in range(CB):
                    for t, (f0, fr) in enumerate(FT):
                        mm = pe.matmul(ps[0:NQ, 6 + e % 2, m * D:(m + 1) * D],
                                       hid[0:fr, e % 2, t, m * NQ:(m + 1) * NQ], w2[0:fr, e, t, :],
                                       start=(t == 0), stop=(t == len(FT) - 1))
                mm.then_inc(e_made, 1)

            def experts(c, first):
                for e in range(E):
                    first_product(c, e, first)
                    if e:
                        second_product(c, e - 1, first)
                    elif not first:
                        second_product(c - 1, E - 1, first)

            experts(0, True)
            with pe.Fori(1, NCH) as c:
                experts(c, False)
            second_product(NCH - 1, E - 1, False)


_OUT = (B, NQ, D)


def kernel(x, ctx_512, g_xattn, g_ffn, L0_xattn_Wq, L0_xattn_Wkv, L0_xattn_Wo, L0_ffn_wqkv, L0_ffn_w1, L0_ffn_w2):
    import concourse.bacc as _bacc
    from concourse.bass_utils import run_bass_kernel_spmd as _run

    def turned(a, *axes):
        return np.ascontiguousarray(np.transpose(a, axes or None))

    order = np.arange(D).reshape(NP, 2, HD).transpose(1, 2, 0).reshape(D)
    num = np.zeros((128, 4, 128), np.float32)
    den = np.zeros((128, 4, 128), np.float32)
    for h in range(H):
        hp, u = h // 2, h % 2
        for d in range(HD):
            num[32 * (hp % 4) + HD * u + d, 2 * (hp // 4) + u, HD * h + d] = 1
            den[32 * (hp % 4) + 16 + HD * u + d, 2 * (hp // 4) + u, HD * h + d] = 1
    mask = np.zeros((D, H), mybir.dt.np(BF16) if hasattr(mybir.dt, "np") else np.float32)
    for p, channel in enumerate(order):
        mask[p, channel // HD] = 1
    x, wkv = np.asarray(x), np.asarray(L0_xattn_Wkv)
    arrays = {
        "x": np.ascontiguousarray(x),
        "ctx_t": turned(np.asarray(ctx_512), 0, 2, 1),
        "g_x": np.asarray(g_xattn), "g_f": np.asarray(g_ffn),
        "wq_t": turned(np.asarray(L0_xattn_Wq)[order]),
        "wk_t": turned(wkv[:D][order]),
        "wv_t": turned(wkv[D:]),
        "wo_t": turned(np.asarray(L0_xattn_Wo)),
        "wr_t": turned(np.asarray(L0_ffn_wqkv)),
        "w1_t": turned(np.asarray(L0_ffn_w1), 2, 0, 1).reshape(D, E * 2 * F),
        "w2_t": turned(np.asarray(L0_ffn_w2), 0, 2, 1),
        "ident": np.eye(128, dtype=np.float32),
        "head_mask": mask,
        "pick_num": num,
        "pick_den": den,
        "rank": np.tile(np.arange(E, 0, -1, dtype=np.float32), (NQ, 1)),
    }
    nc = _bacc.Bacc("TRN2", target_bir_lowering=False, num_devices=1)
    args = [nc.dram_tensor(f"in_{k}", a.shape, mybir.dt.from_np(a.dtype), kind="ExternalInput").ap()
            for k, a in arrays.items()]
    args.append(nc.dram_tensor("out", _OUT, F32, kind="ExternalOutput").ap())
    build(nc, *args)
    r = _run(nc, [{f"in_{k}": a for k, a in arrays.items()}], core_ids=[0])
    return r.results[0]["out"]
```

```python
from contextlib import ExitStack

import numpy as np

import concourse.bass as bass
from concourse import mybir

F32 = mybir.dt.float32
I32 = mybir.dt.int32
U32 = mybir.dt.uint32
BF16 = mybir.dt.bfloat16
ALU = mybir.AluOpType
ACT = mybir.ActivationFunctionType
AX = mybir.AxisListType

B, NQ, D = 32, 100, 128
NK, L = 1444, 64
H, HD = 16, 8
NP = H // 2
E, F = 8, 352
EPS = 1e-5
SCALE = HD ** -0.5
LOWEST = -3.0e38

KT = -(-NK // 128)
ROWS = H * NQ
RT = -(-ROWS // 128)
CH = [482, 482, 480]
CO = [0, 482, 964]
NC = len(CH)
SM = RT * NC
UNITS = 2 * KT
HW = ROWS // 2
PW = 2 * NQ
KPART = [0, 0, 0, 1, 1, 2]
QPART = [0, 1, 2, 0, 1, 0]
UROWS = len(KPART) * HD
KROWS = 2 * UROWS + 2
CB = 4
CT = CB * NQ
NCH = B // CB
FT = [(0, 128), (128, 128), (256, 96)]
TOK = B * NQ
REGION = TOK + 128
TILES = -(-2 * TOK // 128) + E - 1
SPARE = E
PEEL = 4
SLOTS = 4
assert (TILES - 1 - PEEL) % SLOTS == 0
ROW = D + 2
DMA = 16
COPIES = 2 * len(KPART)

AHEAD = 13
PLAN = [[] for _ in range(UNITS)]
for _u, _use in ((3, ("v", 1, 0)), (5, ("v", 1, 1)), (6, ("v", 1, 2)), (7, ("o", -1, 0)), (9, ("k", 2, 0)),
                 (10, ("k", 2, 1)), (11, ("y", -1, 0)), (12, ("k", 2, 2)), (17, ("m", 1, 0))):
    PLAN[_u].append(_use)
_n = AHEAD
for _u in range(UNITS):
    _take = range(_n, _n + 2 - len(PLAN[_u]))
    PLAN[_u] = [("s", 1, m) if m < SM else ("t", 2, m - SM) for m in _take] + PLAN[_u]
    _n = _take.stop
assert _n == SM + AHEAD
FIRST = [("k", 0, n) for n in range(NC)] + [("s", 0, n) for n in range(SM)] + [("k", 1, n) for n in range(NC)] \
    + [("m", 0, 0)] + [("s", 1, n) for n in range(4)] + [("v", 0, n) for n in range(NC)] \
    + [("s", 1, n) for n in range(4, AHEAD)]
ALL = "skvmoyt"


def kinds_of(i):
    return "skvmt" if i == 0 else "svmoy" if i == B - 2 else "oy" if i == B - 1 else ALL


def uses_of(kinds):
    return [use for units in PLAN for use in units if use[0] in kinds]


PACK, _at = {}, 0
for _name, _cols in (("batches", 2 * (B * E + E)), ("before", 128), ("ones", 128), ("region", E), ("fill", E),
                     ("spare", E + SPARE), ("token", 2 * B), ("rows", TILES), ("full", E * (TOK // 128 + 1)),
                     ("upto", E * E)):
    PACK[_name] = (_at, _at + _cols)
    _at += _cols
PACKED = _at
FULL = TOK // 128 + 1


def key_rows(t):
    return min(128, NK - 128 * t)


def score_rows(t):
    return min(128, ROWS - 128 * t)


def build(nc, x, ctx_t, g_x, g_f, wq_t, wk_t, wv_t, wo_t, wr_t, w1_t, w2_t,
          ident, head_mask, pick_num, pick_den, rank, pack, out):
    with ExitStack() as stack:
        def sb(name, shape, dt=F32):
            return stack.enter_context(nc.sbuf_tensor(name, shape, dt))

        def sem(name):
            return stack.enter_context(nc.semaphore(name))

        xs = sb("xs", [NQ, B * D])
        q_part = sb("q_part", [128, 3, B * NQ], BF16)
        ctx = sb("ctx", [L, 2, NK])
        k_full = sb("k_full", [128, NK])
        k_rest = sb("k_rest", [128, NK])
        k_hi = sb("k_hi", [128, 2, NK], BF16)
        k_mid = sb("k_mid", [128, NK], BF16)
        k_lo = sb("k_lo", [128, NK], BF16)
        k_stack = sb("k_stack", [128, 2, NP, NK], BF16)
        q_full = sb("q_full", [128, 2, CT])
        q_rest = sb("q_rest", [128, 2, CT])
        q_stack = sb("q_stack", [KROWS, 2, RT * 128], BF16)
        v_ones = sb("v_ones", [128, 2, KT, NP, 32])
        probs = sb("probs", [128, 4, HW])
        q_block = sb("q_block", [128, 2, H, NQ], BF16)
        maxes = sb("maxes", [128, RT, NC])
        neg_max = sb("neg_max", [128, RT])
        max_row = sb("max_row", [RT, 2, 128], BF16)
        o_sum = sb("o_sum", [128, 4 * NQ])
        den_inv = sb("den_inv", [128, NQ])
        o_norm = sb("o_norm", [128, NQ])
        xn = sb("xn", [NQ, 2, CT * D // NQ])
        wq = sb("wq", [D, D])
        wk = sb("wk", [L, D])
        wv = sb("wv", [L, D])
        wo = sb("wo", [D, D])
        wr = sb("wr", [D, 3 * E])
        idn = sb("idn", [128, 128])
        hmask = sb("hmask", [128, H], BF16)
        pnum = sb("pnum", [128, 4, 128])
        pden = sb("pden", [128, 4, 128])
        rnk = sb("rnk", [NQ, E])
        g_in = sb("g_in", [NQ, 2])
        g_tanh = sb("g_tanh", [NQ, 2])
        stats = sb("stats", [NQ, B * 6])
        mean = sb("mean", [NQ, B])
        rstd = sb("rstd", [NQ, B])
        tmp = sb("tmp", [NQ, 4, B])
        mixed = sb("mixed", [NQ, B, 3 * E])
        route = sb("route", [NQ, 8, B, E])
        pick = sb("pick", [NQ, 6, B])
        place = sb("place", [NQ, 2, B], U32)
        fill_place = sb("fill_place", [128, E], U32)
        table = sb("table", [1, 2, TILES], I32)
        t_gate = sb("t_gate", [128, SLOTS])
        t_dest = sb("t_dest", [128, SLOTS], U32)

        rows_d = nc.dram_tensor("sorted_rows", [E * REGION + SPARE * 128, ROW], F32).ap()
        y_d = nc.dram_tensor("expert_out", [2 * TOK + (E + SPARE) * 128, D], F32).ap()

        xt = probs[:].rearrange("p a b -> p (a b)")
        k_flat = k_stack[:].rearrange("p a b n -> p (a b n)").bitcast(F32)
        w1 = k_flat[:, 0:E * 2 * F]
        w2 = k_flat[:, E * 2 * F:E * (2 * F + len(FT) * D)].rearrange("p (e t d) -> p e t d", e=E, t=len(FT))
        v_flat = v_ones[:].rearrange("p a b c d -> p (a b c d)")
        outer = [v_flat[0:NQ, n * B * E * E:(n + 1) * B * E * E].rearrange("q (b i j) -> q b i j", b=B, i=E)
                 for n in range(3)]
        choice = q_part[:].rearrange("p a n -> p (a n)").bitcast(F32)[0:NQ, 0:B * ROW] \
            .rearrange("q (b r) -> q b r", r=ROW)
        w_end = E * (2 * F + len(FT) * D)
        zeros = k_flat[:, w_end:w_end + (E + SPARE) * ROW].rearrange("p (t r) -> p t r", r=ROW)
        y_in = [k_flat[0:NQ, n * B * D:(n + 1) * B * D] for n in (0, 1)]
        packed = k_full[:, 0:PACKED]

        def const(name, rows=128):
            return packed[0:rows, PACK[name][0]:PACK[name][1]]

        count = k_rest[0:NQ, 0:B * E + E]
        totals = k_rest[:, 264:520].rearrange("p (a n) -> p a n", a=2)
        spot = k_rest[0:NQ, 520:776].rearrange("q (b e) -> q b e", b=B)
        past_end = k_rest[0:1, 776:776 + TILES * E].rearrange("q (s e) -> q s e", e=E)
        q_flat = q_full[:].rearrange("p a n -> p (a n)")
        is_full = q_flat[0:1, 0:E * FULL].rearrange("q (e j) -> q e j", e=E)
        partial = q_flat[0:1, 224:224 + E * E].rearrange("q (e j) -> q e j", e=E)
        e_tiles, e_end, e_jump = (q_flat[0:1, 288 + n * E:288 + (n + 1) * E] for n in range(3))
        jumped, row_of, expert_of = (q_flat[0:1, 320 + n * TILES:320 + (n + 1) * TILES] for n in range(3))
        past_jump = q_rest[:].rearrange("p a n -> p (a n)")[0:1, 0:TILES * E].rearrange("q (s e) -> q s e", e=E)
        room = [0]

        def take(cols, n):
            room[0] += cols * n
            return v_flat[:, room[0] - cols * n:room[0]].rearrange("p (n c) -> p n c", n=n)

        t_row, t_x, t_silu = take(ROW, SLOTS), take(128, 2), take(F, 2)
        t_hid, t_turn, t_y = take(F, 2), take(3 * 128, 2), take(D, SLOTS)

        ps = stack.enter_context(nc.psum_tensor("ps", [128, 8, 512], F32))
        RING, OB = 4, 7

        x_in = sem("x_in")
        const_in = sem("const_in")
        w_in = sem("w_in")
        ctx_in = [sem("ctx_in0"), sem("ctx_in1")]
        k_in = sem("k_in")
        q_in = sem("q_in")
        max_in = sem("max_in")
        cleared = sem("cleared")
        v_step = sem("v_step")
        a_step = sem("a_step")
        v_asks = sem("v_asks")
        tanh_done = sem("tanh_done")
        stats_ready = sem("stats_ready")
        xn_ready = sem("xn_ready")
        xn_turned = sem("xn_turned")
        xt_ready = sem("xt_ready")
        q_made = sem("q_made")
        q_scaled = sem("q_scaled")
        q_split = sem("q_split")
        k_made = sem("k_made")
        k_taken = sem("k_taken")
        k_parted = sem("k_parted")
        v_made = sem("v_made")
        v_taken = sem("v_taken")
        block_ready = sem("block_ready")
        sm_made = sem("sm_made")
        sm_taken = sem("sm_taken")
        neg_ready = sem("neg_ready")
        max_turned = sem("max_turned")
        row_ready = sem("row_ready")
        st_made = sem("st_made")
        exp_done = sem("exp_done")
        pv_done = sem("pv_done")
        o_copied = sem("o_copied")
        nd_made = sem("nd_made")
        inv_ready = sem("inv_ready")
        on_ready = sem("on_ready")
        y_made = sem("y_made")
        y_added = sem("y_added")
        mixed_made = sem("mixed_made")
        mixed_taken = sem("mixed_taken")
        counted = sem("counted")
        totals_made = sem("totals_made")
        totals_ready = sem("totals_ready")
        spots_made = sem("spots_made")
        pack_in = sem("pack_in")
        zeros_ready = sem("zeros_ready")
        spare_out = sem("spare_out")
        first_ready = sem("first_ready")
        first_out = sem("first_out")
        second_ready = sem("second_ready")
        second_out = sem("second_out")
        fill_ready = sem("fill_ready")
        fill_out = sem("fill_out")
        table_ready = sem("table_ready")
        t_row_in = [sem(f"t_row_in{n}") for n in range(SLOTS)]
        t_x_turned = sem("t_x_turned")
        t_x_ready = sem("t_x_ready")
        t_dest_ready = sem("t_dest_ready")
        t_h_made = sem("t_h_made")
        t_silu_done = sem("t_silu_done")
        t_hid_ready = sem("t_hid_ready")
        t_turned = sem("t_turned")
        t_turn_ready = sem("t_turn_ready")
        t_y_made = sem("t_y_made")
        t_y_ready = sem("t_y_ready")
        t_y_out = [sem(f"t_y_out{n}") for n in range(SLOTS)]
        y_back = sem("y_back")
        added = sem("added")
        out_done = sem("out_done")

        block = stack.enter_context(nc.Block())

        def at(i, it, off):
            return i + off

        def ring_read(eng, kind, b, n):
            if kind in "st":
                eng.wait_ge(sm_taken, b * SM + n + 1)
            elif kind == "k":
                eng.wait_ge(k_taken, b * NC + n + 1)
            elif kind == "v":
                eng.wait_ge(v_taken, b * NC + n + 1)
            elif kind == "m":
                eng.wait_ge(row_ready, b * 2 + 2)
            elif kind == "o":
                eng.wait_ge(on_ready, b + 1)
            else:
                eng.wait_ge(y_added, b + 1)

        def batches(eng, body, last=B):
            for i in (0, 1):
                body(i, 0, i, kinds_of(i), kinds_of(i - 1) if i else None)
            with eng.Fori(1, B // 2 - 1) as it:
                for par in (0, 1):
                    body(it * 2 + par, it, par, ALL, ALL)
            for i in (B - 2, B - 1):
                body(i, i // 2, i % 2, kinds_of(i), kinds_of(i - 1))

        def tiles(eng, body, lag=0):
            values = {}
            for s in range(PEEL):
                body(s, s // SLOTS, s % SLOTS, s, values)
            with eng.Fori(0, (TILES - 1 - PEEL) // SLOTS) as it:
                values = {}
                for s in range(PEEL, PEEL + SLOTS):
                    body(it * SLOTS + s, it + s // SLOTS, s % SLOTS, s, values)
            values = {}
            for s in range(TILES - 1, TILES + lag):
                body(s, s // SLOTS, s % SLOTS, s, values)

        @block.sync
        def _(sp):
            step = CB * 2
            for dst, src in ((idn, ident), (wq, wq_t), (wk, wk_t)):
                sp.dma_start(dst[:], src).then_inc(const_in, DMA)
            sp.dma_start(ctx[:, 0, :], ctx_t[0]).then_inc(ctx_in[0], DMA)
            for n in range(0, B, step):
                sp.dma_start(xs[:, n * D:(n + step) * D].rearrange("q (b d) -> q b d", b=step),
                             x[n:n + step].rearrange("b q d -> q b d")).then_inc(x_in, DMA)
            sp.dma_start(ctx[:, 1, :], ctx_t[1]).then_inc(ctx_in[1], DMA)
            for dst, src in ((hmask, head_mask), (wv, wv_t), (wo, wo_t), (wr, wr_t), (rnk, rank),
                             (pnum, pick_num), (pden, pick_den)):
                sp.dma_start(dst[:], src).then_inc(const_in, DMA)
            for n, g in enumerate((g_x, g_f)):
                sp.dma_start(g_in[:, n:n + 1], g.rearrange("(a b) -> a b", a=1).to_broadcast([NQ, 1])) \
                    .then_inc(const_in, DMA)

            def held(value):
                return value if isinstance(value, int) else sp.snap(sp.to_reg(value))

            def stacks(b, par, parts, tokens):
                sp.wait_ge(k_taken, parts)
                sp.wait_ge(k_parted, parts)
                for s, part in enumerate(KPART):
                    src = (k_hi[:, par, :], k_mid[:], k_lo[:])[part]
                    for u in (0, 1):
                        r = u * UROWS + s * HD
                        sp.dma_start(k_stack[r:r + HD, par, :, :], src[64 * u:64 * u + 64, :]).then_inc(k_in, DMA)
                if isinstance(b, int) and b == 0:
                    sp.wait_ge(q_split, 1)
                for s, part in enumerate(QPART):
                    for u in (0, 1):
                        r = u * UROWS + s * HD
                        dst = q_stack[r:r + HD, par, 0:ROWS].rearrange("p (h n) -> p h n", h=NP)
                        sp.dma_start(dst[:, :, u * NQ:(u + 1) * NQ],
                                     q_part[64 * u:64 * u + 64, part, bass.ds(tokens, NQ)]).then_inc(q_in, DMA)

            def max_rows(par, parts):
                sp.wait_ge(row_ready, parts)
                for n in (0, 1):
                    dst = q_stack[2 * UROWS + n:2 * UROWS + n + 1, par, :].rearrange("p (t n) -> p t n", t=RT)
                    sp.dma_start(dst, max_row[:, n, :]).then_inc(max_in, DMA)

            sp.wait_ge(cleared, 6)
            stacks(0, 0, NC, 0)
            sp.wait_ge(v_made, NC)
            max_rows(0, 2)
            sp.wait_ge(q_split, NCH)

            def body(i, it, par, kinds, before):
                if "s" not in kinds:
                    return
                units, copies, copied = held(i * UNITS), held((i + 1) * (COPIES * DMA)), held((i + 1) * (2 * DMA))
                parts, tokens, turned = held((i + 2) * NC), held((i + 1) * NQ), held((i + 2) * 2)
                if "k" in kinds:
                    src = ctx_t[bass.ds(i + 2, 1)].rearrange("a l k -> (a l) k")
                    sp.dma_start(ctx[:, par, :], src).then_inc(ctx_in[par], DMA)
                if "o" in kinds:
                    sp.wait_ge(st_made, units)
                sp.wait_ge(k_in, copies)
                sp.wait_ge(q_in, copies)
                stacks(i + 1, 1 - par, parts, tokens)
                sp.wait_ge(max_in, copied)
                sp.wait_ge(v_made, parts)
                max_rows(1 - par, turned)

            batches(sp, body)
            sp.wait_ge(st_made, B * UNITS)
            sp.dma_start(packed, pack).then_inc(pack_in, DMA)
            sp.dma_start(w1, w1_t).then_inc(w_in, DMA)
            for t, (f0, fr) in enumerate(FT):
                sp.dma_start(w2[0:fr, :, t, :], w2_t[:, f0:f0 + fr, :].rearrange("e f d -> f e d")).then_inc(w_in, DMA)
            sp.wait_ge(zeros_ready, 2)
            sp.dma_start(rows_d[E * REGION:E * REGION + SPARE * 128].rearrange("(t p) r -> p t r", p=128),
                         zeros[:, E:E + SPARE, :]).then_inc(spare_out, DMA)
            sp.wait_ge(spare_out, DMA)
            sp.wait_ge(first_out, B * DMA)
            sp.wait_ge(fill_out, E * DMA)
            sp.wait_ge(second_out, B * DMA)
            sp.wait_ge(table_ready, 2)

            def load_tile(s, turn, slot, step, values):
                row = sp.value_load(table[0:1, 0, bass.ds(s, 1)], min_val=0,
                                    max_val=E * REGION + (SPARE - 1) * 128)
                if not isinstance(s, int) or s >= SLOTS:
                    past = s - (SLOTS - 1)
                    past = past if isinstance(past, int) else held(past)
                    sp.wait_ge(t_x_turned, past)
                    sp.wait_ge(t_dest_ready, past)
                sp.dma_start(t_row[:, slot, :], rows_d[bass.ds(row, 128), :]).then_inc(t_row_in[slot], DMA)

            tiles(sp, load_tile)
            for slot in range(SLOTS):
                sp.wait_ge(t_y_out[slot], len(range(slot, TILES, SLOTS)) * DMA)
            for c in range(NCH):
                for n in (0, 1):
                    sp.dma_start(y_in[n][:, c * CB * D:(c + 1) * CB * D].rearrange("q (b d) -> q b d", b=CB),
                                 y_d[n * TOK + c * CT:n * TOK + (c + 1) * CT].rearrange("(b q) d -> q b d", b=CB)) \
                        .then_inc(y_back, DMA)
            for c in range(NCH):
                sp.wait_ge(added, 2 * c + 2)
                sp.dma_start(out[c * CB:(c + 1) * CB].rearrange("b q d -> q b d"),
                             xs[:, c * CB * D:(c + 1) * CB * D].rearrange("q (b d) -> q b d", b=CB)) \
                    .then_inc(out_done, DMA)
            sp.wait_ge(out_done, NCH * DMA)

        @block.gpsimd
        def _(pool):
            pool.memset(q_stack[:], 0.0).then_inc(cleared, 1)
            pool.memset(maxes[:], 0.0).then_inc(cleared, 1)
            pool.memset(v_ones[:, :, :, :, 2 * HD:32], 1.0).then_inc(cleared, 1)
            pool.wait_ge(cleared, 3)
            pool.memset(v_ones[:, :, KT - 1, :, :], 0.0).then_inc(cleared, 1)
            pool.wait_ge(cleared, 4)
            pool.memset(v_ones[0:key_rows(KT - 1), :, KT - 1, :, 2 * HD:32], 1.0).then_inc(cleared, 1)
            pool.memset(k_stack[2 * UROWS:KROWS, :, :, :], 1.0).then_inc(cleared, 1)

            def block_q(b, par):
                q = q_part[:, 0, bass.ds(b * NQ, NQ)]
                pool.tensor_tensor(q_block[:, par, :, :], q.unsqueeze(1).to_broadcast([128, H, NQ]),
                                   hmask[:].unsqueeze(2).to_broadcast([128, H, NQ]), ALU.mult).then_inc(block_ready, 1)

            def part_k(b, par):
                pool.wait_ge(k_taken, (b + 1) * NC)
                if not (isinstance(b, int) and b == 0):
                    pool.wait_ge(k_in, b * COPIES * DMA)
                pool.tensor_tensor(k_mid[:], k_full[:], k_hi[:, par, :], ALU.subtract).then_inc(k_parted, 1)
                pool.tensor_tensor(k_rest[:], k_full[:], k_hi[:, par, :], ALU.subtract).then_inc(k_parted, 1)
                pool.wait_ge(k_parted, b * 3 + 2)
                pool.tensor_tensor(k_lo[:], k_rest[:], k_mid[:], ALU.subtract).then_inc(k_parted, 1)

            pool.wait_ge(const_in, DMA * 12)
            part_k(0, 0)
            pool.wait_ge(q_scaled, 1)
            block_q(0, 0)
            block_q(1, 1)
            part_k(1, 1)
            pool.wait_ge(q_scaled, NCH)

            def body(i, it, par, kinds, before):
                if "k" in kinds:
                    pool.wait_ge(sm_made, (i + 1) * SM)
                    block_q(i + 2, par)
                    part_k(i + 2, par)

            batches(pool, body)

            def scatter(dst, where, src, done):
                pool.indirect_dma_start(dst, bass.IndirectOffsetOnAxis(ap=where, axis=0), src, None) \
                    .then_inc(done, DMA)

            pool.wait_ge(st_made, B * UNITS)
            pool.memset(zeros, 0.0).then_inc(zeros_ready, 1)
            pool.wait_ge(pack_in, DMA)
            pool.wait_ge(zeros_ready, 1)
            pool.tensor_copy(zeros[:, :, D + 1], const("spare")).then_inc(zeros_ready, 1)
            pool.wait_ge(first_ready, 2)
            for b in range(B):
                scatter(rows_d, place[:, 0, b:b + 1], choice[:, b, :], first_out)
            pool.wait_ge(zeros_ready, 2)
            pool.wait_ge(fill_ready, 1)
            for e in range(E):
                scatter(rows_d, fill_place[:, e:e + 1], zeros[:, e, :], fill_out)
            pool.wait_ge(second_ready, 2)
            for b in range(B):
                scatter(rows_d, place[:, 1, b:b + 1], choice[:, b, :], second_out)

            put = pool.alloc_register("put")
            pool.reg_mov(put, PEEL + 1)

            def put_tile(s, turn, slot, step, values):
                if isinstance(s, int):
                    pool.wait_ge(t_y_ready, s + 1)
                else:
                    pool.wait_ge(t_y_ready, put)
                    pool.reg_add(put, put, 1)
                scatter(y_d, t_dest[:, slot:slot + 1], t_y[:, slot, :], t_y_out[slot])

            tiles(pool, put_tile)

        @block.scalar
        def _(act):
            act.wait_ge(const_in, DMA * 12)
            act.wait_ge(cleared, 6)
            act.activation(g_tanh[:], g_in[:], ACT.Tanh).then_inc(tanh_done, 1)

            def root(phase):
                act.wait_ge(v_asks, 1 if phase == 0 else 2)
                act.activation(tmp[:, 3, :], tmp[:, 2, :], ACT.Sqrt).then_inc(a_step, 1)

            def take_xt(phase, c):
                act.wait_ge(xn_turned, phase * NCH + c + 1)
                act.activation(xt[:, c * CT:(c + 1) * CT], ps[:, c % 2, 0:CT], ACT.Copy).then_inc(xt_ready, 1)

            def take_first(uses):
                for n_use, (kind, b, n) in enumerate(uses):
                    if kind == "k":
                        take_k(b, 0, b % 2, n, RING + n_use % 3)
                    elif kind == "v":
                        take_v(b, b % 2, n, RING + n_use % 3)

            def take_q(c):
                if c >= 2:
                    act.wait_ge(q_split, c - 1)
                act.wait_ge(q_made, c + 1)
                src = ps[:, 2 + c % 2, 0:CT]
                act.activation(q_full[:, c % 2, :], src, ACT.Copy, scale=SCALE)
                act.activation(q_part[:, 0, c * CT:(c + 1) * CT], src, ACT.Copy, scale=SCALE).then_inc(q_scaled, 1)

            def take_k(b, it, par, n, bank):
                act.wait_ge(k_made, b * NC + n + 1)
                if n == 0 and not isinstance(b, int) or n == 0 and b >= 1:
                    act.wait_ge(k_parted, b * 3)
                if n == 0 and (not isinstance(b, int) or b >= 2):
                    act.wait_ge(sm_made, (b - 1) * SM)
                    act.wait_ge(k_in, (b - 1) * COPIES * DMA)
                src = ps[:, bank, 0:CH[n]]
                act.activation(k_full[:, CO[n]:CO[n] + CH[n]], src, ACT.Copy)
                act.activation(k_hi[:, par, CO[n]:CO[n] + CH[n]], src, ACT.Copy).then_inc(k_taken, 1)

            def take_v(b, par, n, bank):
                act.wait_ge(v_made, b * NC + n + 1)
                if n == 0 and (not isinstance(b, int) or b >= 2):
                    act.wait_ge(pv_done, (b - 1) * UNITS)
                full = sum(key_rows(t) == 128 for t in range(4 * n, 4 * n + 4))
                src = ps[:, bank, :].rearrange("p (t h c) -> p t h c", t=4, h=NP)
                dst = v_ones[:, par, 4 * n:4 * n + 4, :, 0:2 * HD]
                last = act.activation(dst[:, 0:full], src[:, 0:full], ACT.Copy)
                if full < 4:
                    r = key_rows(KT - 1)
                    last = act.activation(dst[0:r, full], src[0:r, full], ACT.Copy)
                last.then_inc(v_taken, 1)

            take_first(FIRST[:NC])
            root(0)
            for c in range(NCH):
                take_xt(0, c)
                if c >= 1:
                    take_q(c - 1)
            take_q(NCH - 1)
            take_first([("", 0, 0)] * NC + FIRST[NC:])
            used = [len(FIRST)]

            def copy_o(b, last=False):
                act.wait_ge(pv_done, (b + 1) * UNITS)
                if not isinstance(b, int) or b >= 1:
                    act.wait_ge(nd_made, b)
                act.activation(o_sum[:], ps[:, OB, 0:4 * NQ], ACT.Copy).then_inc(o_copied, 1)

            def body(i, it, par, kinds, before):
                for u in range(UNITS):
                    act.wait_ge(st_made, i * UNITS + u + 1)
                    if not isinstance(i, int) or i * UNITS + u >= 4:
                        act.wait_ge(pv_done, i * UNITS + u - 3)
                    r = key_rows(u // 2)
                    act.activation(probs[0:r, u % 4, :].rearrange("p (a n) -> p a n", a=2),
                                   ps[0:r, 2 * (u % 2):2 * (u % 2) + 2, 0:CT], ACT.Exp).then_inc(exp_done, 1)
                    if u == 1 and "o" in kinds:
                        copy_o(i - 1)
                    for kind, off, n in PLAN[u]:
                        if kind in kinds:
                            bank = RING + used[0] % 3
                            used[0] += 1
                            if kind == "k":
                                take_k(i + off, it, par, n, bank)
                            elif kind == "v":
                                take_v(i + off, 1 - par, n, bank)

            batches(act, body)
            copy_o(B - 1)
            root(1)
            for c in range(NCH):
                take_xt(1, c)
            for g in range(2):
                act.wait_ge(mixed_made, g + 1)
                act.activation(mixed[:, g * B // 2:(g + 1) * B // 2, :],
                               ps[0:NQ, 2 + g, 0:B // 2 * 3 * E].rearrange("q (b e) -> q b e", b=B // 2),
                               ACT.Copy).then_inc(mixed_taken, 1)
            act.wait_ge(v_asks, 3)
            act.activation(outer[1], outer[0], ACT.Exp).then_inc(a_step, 1)
            act.wait_ge(v_asks, 4)
            act.activation(pick[:, 3, :], pick[:, 2, :], ACT.Exp).then_inc(a_step, 1)

            act.wait_ge(totals_made, 1)
            act.activation(totals, ps[:, 4, 0:256].rearrange("p (a n) -> p a n", a=2), ACT.Copy) \
                .then_inc(totals_ready, 1)

            def take_x(s):
                act.wait_ge(t_x_turned, s + 1)
                if not isinstance(s, int) or s >= 2:
                    act.wait_ge(t_h_made, s - 1)
                par = carried["slot"] % 2
                act.activation(t_x[:, par, :], ps[:, 6, 0:128], ACT.Copy).then_inc(t_x_ready, 1)

            carried = {}

            def act_tile(s, turn, slot, step, values):
                par = slot % 2
                if isinstance(s, int) and s == 0:
                    carried["slot"] = 0
                    take_x(0)
                if not isinstance(s, int) or s + 1 < TILES:
                    carried["slot"] = slot + 1
                    take_x(s + 1)
                if not isinstance(s, int) or s < TILES:
                    act.wait_ge(t_h_made, s + 1)
                    if not isinstance(s, int) or s >= 2:
                        act.wait_ge(t_hid_ready, s - 1)
                    act.activation(t_silu[:, par, :], ps[:, 2 * par, 0:F], ACT.Silu).then_inc(t_silu_done, 1)
                if not isinstance(s, int) or s >= 1:
                    act.wait_ge(t_turned, s)
                    if not isinstance(s, int) or s >= 3:
                        act.wait_ge(t_y_made, s - 2)
                    act.activation(t_turn[:, 1 - par, 0:256], ps[:, 5 - par, 0:256], ACT.Copy)
                    fr = FT[2][1]
                    act.activation(t_turn[0:fr, 1 - par, 256:384], ps[0:fr, 5 - par, 256:384], ACT.Copy) \
                        .then_inc(t_turn_ready, 1)

            tiles(act, act_tile, lag=1)

        @block.vector
        def _(dve):
            steps = [0]

            def step(ins):
                ins.then_inc(v_step, 1)
                steps[0] += 1
                dve.wait_ge(v_step, steps[0])

            def norm(phase):
                dve.wait_ge(stats_ready, (phase + 1) * B)
                st = stats[:].rearrange("q (b s) -> q s b", s=6)
                step(dve.tensor_tensor(tmp[:, 0, :], st[:, 1, :], st[:, 4, :], ALU.add))
                step(dve.tensor_scalar(mean[:], tmp[:, 0, :], 0.5, None, ALU.mult))
                step(dve.tensor_tensor(tmp[:, 1, :], st[:, 1, :], st[:, 4, :], ALU.subtract))
                step(dve.tensor_tensor(tmp[:, 0, :], tmp[:, 1, :], tmp[:, 1, :], ALU.mult))
                step(dve.scalar_tensor_tensor(tmp[:, 1, :], tmp[:, 0, :], D / 4, st[:, 2, :], ALU.mult, ALU.add))
                step(dve.tensor_tensor(tmp[:, 0, :], tmp[:, 1, :], st[:, 5, :], ALU.add))
                dve.tensor_scalar(tmp[:, 2, :], tmp[:, 0, :], 1.0 / D, EPS, ALU.mult, ALU.add).then_inc(v_asks, 1)
                dve.wait_ge(a_step, 1 if phase == 0 else 2)
                step(dve.reciprocal(tmp[:, 0, :], tmp[:, 3, :]))
                step(dve.tensor_tensor(tmp[:, 1, :], tmp[:, 0, :], tmp[:, 0, :], ALU.mult))
                step(dve.tensor_tensor(tmp[:, 3, :], tmp[:, 1, :], tmp[:, 2, :], ALU.mult))
                step(dve.tensor_scalar(tmp[:, 1, :], tmp[:, 3, :], -0.5, 1.5, ALU.mult, ALU.add))
                step(dve.tensor_tensor(rstd[:], tmp[:, 0, :], tmp[:, 1, :], ALU.mult))

            def norm_chunk(phase, c):
                n = phase * NCH + c
                if phase == 0 and c >= 2:
                    dve.wait_ge(xn_turned, c - 1)
                for t in range(CB):
                    b = c * CB + t
                    ins = dve.tensor_scalar(choice[:, b, 0:D] if phase else xn[:, c % 2, t * D:(t + 1) * D], xs[:, b * D:(b + 1) * D],
                                            mean[:, b:b + 1], rstd[:, b:b + 1], ALU.subtract, ALU.mult)
                ins.then_inc(xn_ready, 1)

            def split_q(c):
                of = slice(c * CT, (c + 1) * CT)
                dve.wait_ge(q_scaled, c + 1)
                full, rest = q_full[:, c % 2, :], q_rest[:, c % 2, :]
                step(dve.tensor_tensor(rest, full, q_part[:, 0, of], ALU.subtract))
                step(dve.tensor_copy(q_part[:, 1, of], rest))
                dve.tensor_tensor(q_part[:, 2, of], rest, q_part[:, 1, of], ALU.subtract).then_inc(q_split, 1)

            def statistics(b):
                dve.bn_stats(stats[:, bass.ds(b * 6, 6)], xs[:, bass.ds(b * D, D)]).then_inc(stats_ready, 1)

            dve.wait_ge(x_in, (B // CB // 2) * DMA)
            with dve.Fori(0, B) as b:
                statistics(b)
            norm(0)
            for c in range(NCH):
                norm_chunk(0, c)
                if c >= 1:
                    split_q(c - 1)
            split_q(NCH - 1)

            def take_max(b, n, bank):
                t, c = n // NC, n % NC
                r = score_rows(t)
                dve.wait_ge(sm_made, b * SM + n + 1)
                if n == 0 and (not isinstance(b, int) or b >= 1):
                    dve.wait_ge(neg_ready, b)
                dve.tensor_reduce(maxes[0:r, t, c:c + 1], ps[0:r, bank, 0:CH[c]], AX.X, ALU.max).then_inc(sm_taken, 1)
                if n == SM - 1:
                    dve.wait_ge(sm_taken, b * SM + SM)
                    dve.tensor_reduce(neg_max[:], maxes[:], AX.X, ALU.max, negate=True).then_inc(neg_ready, 1)

            def part_max(b, bank):
                dve.wait_ge(max_turned, b + 1)
                if not isinstance(b, int) or b >= 1:
                    dve.wait_ge(max_in, b * 2 * DMA)
                dve.tensor_copy(max_row[:, 0, :], ps[0:RT, bank, 0:128]).then_inc(row_ready, 1)
                dve.wait_ge(row_ready, b * 2 + 1)
                dve.tensor_tensor(max_row[:, 1, :], ps[0:RT, bank, 0:128], max_row[:, 0, :], ALU.subtract) \
                    .then_inc(row_ready, 1)

            def divide(b, bank):
                dve.wait_ge(nd_made, b + 1)
                dve.reciprocal(den_inv[:], ps[:, bank, 0:NQ]).then_inc(inv_ready, 1)
                dve.wait_ge(inv_ready, b + 1)
                if not isinstance(b, int) or b >= 1:
                    dve.wait_ge(y_made, b)
                dve.tensor_tensor(o_norm[:], ps[:, bank, 128:128 + NQ], den_inv[:], ALU.mult).then_inc(on_ready, 1)

            def add_y(b, bank):
                dve.wait_ge(y_made, b + 1)
                row = xs[:, bass.ds(b * D, D)]
                dve.scalar_tensor_tensor(row, ps[0:NQ, bank, 0:D], g_tanh[:, 0:1], row, ALU.mult, ALU.add) \
                    .then_inc(y_added, 1)
                dve.wait_ge(y_added, b + 1)
                statistics(b)

            dve.wait_ge(cleared, 6)
            dve.wait_ge(tanh_done, 1)
            used = [0]

            def take(kind, b, n):
                bank = RING + used[0] % 3
                used[0] += 1
                if kind in "st":
                    take_max(b, n, bank)
                elif kind == "m":
                    part_max(b, bank)
                elif kind == "o":
                    divide(b, bank)
                elif kind == "y":
                    add_y(b, bank)

            for kind, b, n in FIRST:
                take(kind, b, n)

            def body(i, it, par, kinds, before):
                for kind, off, n in uses_of(kinds):
                    take(kind, i + off, n)

            batches(dve, body)
            take("o", B - 1, 0)
            take("y", B - 1, 0)

            norm(1)
            for c in range(NCH):
                norm_chunk(1, c)
            dve.wait_ge(mixed_taken, 2)
            q, k, v = (mixed[:, :, n * E:(n + 1) * E] for n in range(3))
            wide = [NQ, B, E, E]
            step(dve.tensor_tensor(outer[2], q.unsqueeze(3).to_broadcast(wide), k.unsqueeze(2).to_broadcast(wide),
                                   ALU.mult))
            step(dve.tensor_reduce(route[:, 0, :, :], outer[2], AX.X, ALU.max))
            dve.tensor_tensor(outer[0], outer[2], route[:, 0, :, :].unsqueeze(3).to_broadcast(wide), ALU.subtract) \
                .then_inc(v_asks, 1)
            dve.wait_ge(a_step, 3)
            step(dve.tensor_reduce(route[:, 1, :, :], outer[1], AX.X, ALU.add))
            step(dve.tensor_tensor(outer[2], outer[1], v.unsqueeze(2).to_broadcast(wide), ALU.mult))
            step(dve.tensor_reduce(route[:, 2, :, :], outer[2], AX.X, ALU.add))
            step(dve.reciprocal(route[:, 3, :, :], route[:, 1, :, :]))
            logits = route[:, 0, :, :]
            step(dve.tensor_tensor(logits, route[:, 2, :, :], route[:, 3, :, :], ALU.mult))

            def over_e(t):
                return t.unsqueeze(2).to_broadcast([NQ, B, E])

            def best(values, chosen, top):
                step(dve.tensor_reduce(top, values, AX.X, ALU.max))
                step(dve.tensor_tensor(route[:, 4, :, :], values, over_e(top), ALU.is_equal))
                step(dve.tensor_tensor(route[:, 5, :, :], route[:, 4, :, :],
                                       rnk[:].unsqueeze(1).to_broadcast([NQ, B, E]), ALU.mult))
                step(dve.tensor_reduce(pick[:, 4, :], route[:, 5, :, :], AX.X, ALU.max))
                step(dve.tensor_tensor(chosen, route[:, 5, :, :], over_e(pick[:, 4, :]), ALU.is_equal))

            best(logits, route[:, 1, :, :], pick[:, 0, :])
            step(dve.scalar_tensor_tensor(route[:, 3, :, :], route[:, 1, :, :], LOWEST, logits, ALU.mult, ALU.add))
            best(route[:, 3, :, :], route[:, 2, :, :], pick[:, 1, :])
            dve.tensor_tensor(pick[:, 2, :], pick[:, 1, :], pick[:, 0, :], ALU.subtract).then_inc(v_asks, 1)
            dve.wait_ge(a_step, 4)
            step(dve.tensor_scalar(pick[:, 4, :], pick[:, 3, :], 1.0, None, ALU.add))
            step(dve.reciprocal(pick[:, 5, :], pick[:, 4, :]))
            step(dve.tensor_scalar(pick[:, 4, :], pick[:, 5, :], g_tanh[:, 1:2], None, ALU.mult))
            step(dve.tensor_tensor(pick[:, 5, :], pick[:, 4, :], pick[:, 3, :], ALU.mult))
            dve.memset(count[:, B * E:], 0.0).then_inc(counted, 1)
            dve.tensor_tensor(count[:, 0:B * E].rearrange("q (b e) -> q b e", b=B), route[:, 1, :, :],
                              route[:, 2, :, :], ALU.add).then_inc(counted, 1)
            dve.wait_ge(pack_in, DMA)
            first, second = (const("token", NQ)[:, n * B:(n + 1) * B] for n in (0, 1))
            dve.tensor_copy(choice[:, :, D], pick[:, 4, :]).then_inc(first_ready, 1)
            step(dve.tensor_copy(choice[:, :, D + 1], first))
            dve.wait_ge(spots_made, 1)
            step(dve.tensor_tensor(spot, ps[0:NQ, 5, 0:B * E].rearrange("q (b e) -> q b e", b=B),
                                   const("region", NQ).unsqueeze(1).to_broadcast([NQ, B, E]), ALU.add))
            step(dve.tensor_tensor(route[:, 4, :, :], route[:, 1, :, :], spot, ALU.mult))
            step(dve.tensor_reduce(pick[:, 0, :], route[:, 4, :, :], AX.X, ALU.add))
            dve.tensor_copy(place[:, 0, :], pick[:, 0, :]).then_inc(first_ready, 1)
            dve.tensor_tensor(fill_place[:], ps[:, 5, B * E:B * E + E], const("fill"), ALU.add).then_inc(fill_ready, 1)
            step(dve.tensor_tensor(route[:, 5, :, :], route[:, 2, :, :], spot, ALU.mult))
            step(dve.tensor_reduce(pick[:, 1, :], route[:, 5, :, :], AX.X, ALU.add))
            step(dve.tensor_copy(place[:, 1, :], pick[:, 1, :]))

            step(dve.tensor_tensor(is_full, ps[0:1, 5, B * E:B * E + E].unsqueeze(2).to_broadcast([1, E, FULL]),
                                   const("full", 1).rearrange("q (e j) -> q e j", e=E), ALU.is_gt))
            step(dve.tensor_reduce(e_tiles, is_full, AX.X, ALU.add))
            step(dve.tensor_tensor(partial, e_tiles.unsqueeze(1).to_broadcast([1, E, E]),
                                   const("upto", 1).rearrange("q (e j) -> q e j", e=E), ALU.mult))
            step(dve.tensor_reduce(e_end, partial, AX.X, ALU.add))
            step(dve.tensor_scalar(e_jump, e_tiles, -128.0, float(REGION), ALU.mult, ALU.add))
            over_t = [1, TILES, E]
            step(dve.tensor_scalar(expert_of, const("rows", 1), 1.0 / 128, None, ALU.mult))
            step(dve.tensor_tensor(past_end, expert_of.unsqueeze(2).to_broadcast(over_t),
                                   e_end.unsqueeze(1).to_broadcast(over_t), ALU.is_ge))
            step(dve.tensor_tensor(past_jump, past_end, e_jump.unsqueeze(1).to_broadcast(over_t), ALU.mult))
            step(dve.tensor_reduce(jumped, past_jump, AX.X, ALU.add))
            dve.tensor_tensor(table[:, 0, :], jumped, const("rows", 1), ALU.add).then_inc(table_ready, 1)
            step(dve.tensor_reduce(row_of, past_end, AX.X, ALU.add))
            dve.tensor_scalar(table[:, 1, :], row_of, float(E - 1), None, ALU.min).then_inc(table_ready, 1)

            dve.wait_ge(first_out, B * DMA)
            dve.tensor_copy(choice[:, :, D], pick[:, 5, :]).then_inc(second_ready, 1)
            dve.tensor_copy(choice[:, :, D + 1], second).then_inc(second_ready, 1)

            def take_dest(s, turn, slot):
                dve.wait_ge(t_row_in[slot], (turn + 1) * DMA)
                if not isinstance(s, int) or s >= SLOTS:
                    dve.wait_ge(t_y_out[slot], turn * DMA)
                step(dve.tensor_copy(t_gate[:, slot:slot + 1], t_row[:, slot, D:D + 1]))
                dve.tensor_copy(t_dest[:, slot:slot + 1], t_row[:, slot, D + 1:D + 2]).then_inc(t_dest_ready, 1)

            def dve_tile(s, turn, slot, step, values):
                par = slot % 2
                if not isinstance(s, int) or s < TILES:
                    take_dest(s, turn, slot)
                    dve.wait_ge(t_silu_done, s + 1)
                    if not isinstance(s, int) or s >= 2:
                        dve.wait_ge(t_turned, s - 1)
                    dve.tensor_tensor(t_hid[:, par, :], t_silu[:, par, :], ps[:, 2 * par + 1, 0:F], ALU.mult) \
                        .then_inc(t_hid_ready, 1)
                if not isinstance(s, int) or s >= 2:
                    last = (slot + 2) % SLOTS
                    dve.wait_ge(t_y_made, s - 1)
                    dve.tensor_scalar(t_y[:, last, :], ps[:, 7, 0:D], t_gate[:, last:last + 1], None,
                                      ALU.mult).then_inc(t_y_ready, 1)

            tiles(dve, dve_tile, lag=2)

            for c in range(NCH):
                if c % 2 == 0:
                    dve.wait_ge(y_back, NCH * 2 * DMA)
                for n in (0, 1):
                    at_ = slice(c * CB * D, (c + 1) * CB * D)
                    if n:
                        dve.wait_ge(added, 2 * c + 1)
                    dve.tensor_tensor(xs[:, at_], xs[:, at_], y_in[n][:, at_], ALU.add).then_inc(added, 1)

        @block.tensor
        def _(pe):
            def turn_chunk(phase, c):
                pe.wait_ge(xn_ready, phase * NCH + c + 1)
                if phase or c >= 2:
                    pe.wait_ge(xt_ready, phase * NCH + c - 1)
                for t in range(CB):
                    mm = pe.transpose(ps[:, c % 2, t * NQ:(t + 1) * NQ],
                                      choice[:, c * CB + t, 0:D] if phase else xn[:, c % 2, t * D:(t + 1) * D],
                                      idn[0:NQ, 0:NQ])
                mm.then_inc(xn_turned, 1)

            def make_q(c):
                pe.wait_ge(xt_ready, c + 1)
                if c >= 2:
                    pe.wait_ge(q_scaled, c - 1)
                pe.matmul(ps[:, 2 + c % 2, 0:CT], wq[:], xt[:, c * CT:(c + 1) * CT], start=True, stop=True) \
                    .then_inc(q_made, 1)

            def make_k(b, it, par, n, bank):
                if n == 0:
                    pe.wait_ge(ctx_in[par], (it + 1) * DMA)
                pe.matmul(ps[:, bank, 0:CH[n]], wk[:], ctx[:, par, CO[n]:CO[n] + CH[n]], start=True, stop=True) \
                    .then_inc(k_made, 1)

            def make_v(par, n, bank):
                for t in range(4 * n, 4 * n + 4):
                    r = key_rows(t)
                    mm = pe.matmul(ps[0:r, bank, (t % 4) * D:(t % 4 + 1) * D], ctx[:, par, t * 128:t * 128 + r],
                                   wv[:], start=True, stop=True)
                mm.then_inc(v_made, 1)

            def make_scores(b, par, n, bank):
                t, c = n // NC, n % NC
                r = score_rows(t)
                if t == 0:
                    pe.wait_ge(k_taken, b * NC + c + 1)
                if n == 0:
                    pe.wait_ge(block_ready, b + 1)
                rows = q_block[:, par, :, :].rearrange("p h n -> p (h n)")[:, t * 128:t * 128 + r]
                pe.matmul(ps[0:r, bank, 0:CH[c]], rows, k_hi[:, par, CO[c]:CO[c] + CH[c]],
                          start=True, stop=True).then_inc(sm_made, 1)

            def turn_max(b, bank):
                pe.wait_ge(neg_ready, b + 1)
                pe.transpose(ps[0:RT, bank, 0:128], neg_max[:], idn[:]).then_inc(max_turned, 1)

            def gather(b, bank):
                pe.wait_ge(o_copied, b + 1)
                for pick_, at_ in ((pden, 0), (pnum, 128)):
                    for n in range(4):
                        mm = pe.matmul(ps[:, bank, at_:at_ + NQ], pick_[:, n, :], o_sum[:, n * NQ:(n + 1) * NQ],
                                       start=(n == 0), stop=(n == 3))
                mm.then_inc(nd_made, 1)

            def make_y(b, bank):
                pe.wait_ge(on_ready, b + 1)
                pe.matmul(ps[0:NQ, bank, 0:D], o_norm[:], wo[:], start=True, stop=True).then_inc(y_made, 1)

            def make(kind, b, it, par, n, bank):
                if kind in "st":
                    make_scores(b, par, n, bank)
                elif kind == "k":
                    make_k(b, it, par, n, bank)
                elif kind == "v":
                    make_v(par, n, bank)
                elif kind == "m":
                    turn_max(b, bank)
                elif kind == "o":
                    gather(b, bank)
                else:
                    make_y(b, bank)

            used = [0]
            pe.wait_ge(const_in, DMA * 12)
            for n_use, (kind, b, n) in enumerate(FIRST):
                if n_use == NC:
                    for c in range(NCH):
                        turn_chunk(0, c)
                        if c >= 1:
                            make_q(c - 1)
                    make_q(NCH - 1)
                if n_use >= 3:
                    ring_read(pe, *FIRST[n_use - 3])
                make(kind, b, 0, b % 2, n, RING + n_use % 3)
            used[0] = len(FIRST)

            def scores(i, par, u):
                t, half = u // 2, u % 2
                r = key_rows(t)
                if u == 0:
                    pe.wait_ge(k_in, (i + 1) * COPIES * DMA)
                    pe.wait_ge(q_in, (i + 1) * COPIES * DMA)
                    pe.wait_ge(max_in, (i + 1) * 2 * DMA)
                if not isinstance(i, int) or i * UNITS + u >= 2:
                    pe.wait_ge(exp_done, i * UNITS + u - 1)
                for n in range(4):
                    hp = 4 * half + n
                    mm = pe.matmul(ps[0:r, 2 * (u % 2) + n // 2, (n % 2) * PW:(n % 2 + 1) * PW],
                                   k_stack[0:KROWS, par, hp, t * 128:t * 128 + r],
                                   q_stack[0:KROWS, par, hp * PW:(hp + 1) * PW], start=True, stop=True)
                mm.then_inc(st_made, 1)

            def product(i, par, u):
                t, half = u // 2, u % 2
                pe.wait_ge(exp_done, i * UNITS + u + 1)
                if u == 0:
                    pe.wait_ge(v_taken, (i + 1) * NC)
                    if not isinstance(i, int) or i >= 1:
                        pe.wait_ge(o_copied, i)
                for n in range(4):
                    mm = pe.matmul(ps[32 * n:32 * n + 32, OB, half * PW:(half + 1) * PW],
                                   v_ones[:, par, t, 4 * half + n, :], probs[:, u % 4, n * PW:(n + 1) * PW],
                                   start=(u == 0), stop=(t == KT - 1), skip_group_check=True)
                mm.then_inc(pv_done, 1)

            def body(i, it, par, kinds, before):
                uses = uses_of(kinds)
                past = [(k, o - 1, n) for k, o, n in uses_of(before)[-3:]] if before else \
                    [(k, o, n) for k, o, n in FIRST[-3:]]
                line = past + uses
                if len(line) < len(past) + 1:
                    line = past
                at_use = [3]
                for u in range(UNITS):
                    scores(i, par, u)
                    if u >= 2:
                        product(i, par, u - 2)
                    elif not isinstance(i, int) or i >= 1:
                        product(i - 1, 1 - par, UNITS - 2 + u)
                    for kind, off, n in PLAN[u]:
                        if kind in kinds:
                            k_, o_, n_ = line[at_use[0] - 3]
                            ring_read(pe, k_, i + o_, n_)
                            make(kind, i + off, it + 1, par if kind in "kt" else 1 - par, n, RING + used[0] % 3)
                            at_use[0] += 1
                            used[0] += 1

            batches(pe, body)
            for u in (UNITS - 2, UNITS - 1):
                product(B - 1, 1, u)
            ring_read(pe, "v", B - 1, NC - 1)
            gather(B - 1, RING + used[0] % 3)
            used[0] += 1
            make_y(B - 1, RING + used[0] % 3)

            def mix(c):
                pe.wait_ge(xt_ready, NCH + c + 1)
                for b in range(c * CB, (c + 1) * CB):
                    n = b % (B // 2)
                    mm = pe.matmul(ps[0:NQ, 2 + b // (B // 2), n * 3 * E:(n + 1) * 3 * E],
                                   xt[:, b * NQ:(b + 1) * NQ], wr[:], start=True, stop=True)
                if c % (NCH // 2) == NCH // 2 - 1:
                    mm.then_inc(mixed_made, 1)

            for c in range(NCH):
                turn_chunk(1, c)
                if c >= 1:
                    mix(c - 1)
            mix(NCH - 1)

            pe.wait_ge(pack_in, DMA)
            pe.wait_ge(counted, 2)
            pe.wait_ge(y_added, B)
            for n in (0, 1):
                mm = pe.matmul(ps[:, 4, n * 128:(n + 1) * 128], count[:, n * 128:(n + 1) * 128], const("ones", NQ),
                               start=True, stop=True)
            mm.then_inc(totals_made, 1)
            pe.wait_ge(totals_ready, 1)
            cols = B * E + E
            for n in (0, 1):
                pe.matmul(ps[:, 5, 0:cols], totals[:, n, :], const("batches")[:, n * cols:(n + 1) * cols],
                          start=(n == 0), stop=False)
            pe.matmul(ps[:, 5, 0:cols], const("before", NQ), count, start=False, stop=True) \
                .then_inc(spots_made, 1)

            pe.wait_ge(w_in, (1 + len(FT)) * DMA)
            pe.wait_ge(table_ready, 2)

            def expert(values, s, key):
                if key not in values:
                    values[key] = pe.value_load(table[0:1, 1, bass.ds(s, 1)], min_val=0, max_val=E - 1)
                return values[key]

            def turn_x(s, turn, slot):
                pe.wait_ge(t_row_in[slot], (turn + 1) * DMA)
                if not isinstance(s, int) or s >= 1:
                    pe.wait_ge(t_x_ready, s)
                pe.transpose(ps[:, 6, 0:128], t_row[:, slot, 0:D], idn[:]).then_inc(t_x_turned, 1)

            def pe_tile(s, turn, slot, step, values):
                par = slot % 2
                if isinstance(s, int) and s == 0:
                    turn_x(0, 0, 0)
                if not isinstance(s, int) or s + 1 < TILES:
                    turn_x(s + 1, turn + (slot + 1) // SLOTS, (slot + 1) % SLOTS)
                if not isinstance(s, int) or s < TILES:
                    e = expert(values, s, step)
                    pe.wait_ge(t_x_ready, s + 1)
                    if not isinstance(s, int) or s >= 2:
                        pe.wait_ge(t_hid_ready, s - 1)
                    for half in (0, 1):
                        mm = pe.matmul(ps[:, 2 * par + half, 0:F], t_x[:, par, :],
                                       w1[:, bass.ds(e * (2 * F) + half * F, F)], start=True, stop=True)
                    mm.then_inc(t_h_made, 1)
                if not isinstance(s, int) or s >= 2:
                    e = expert(values, s - 2, step - 2)
                    pe.wait_ge(t_turn_ready, s - 1)
                    if not isinstance(s, int) or s >= 3:
                        pe.wait_ge(t_y_ready, s - 2)
                    for t, (f0, fr) in enumerate(FT):
                        mm = pe.matmul(ps[:, 7, 0:D], t_turn[0:fr, par, t * 128:(t + 1) * 128],
                                       k_flat[0:fr, bass.ds(e * (len(FT) * D) + (E * 2 * F + t * D), D)],
                                       start=(t == 0), stop=(t == len(FT) - 1))
                    mm.then_inc(t_y_made, 1)
                if not isinstance(s, int) or 1 <= s <= TILES:
                    pe.wait_ge(t_hid_ready, s)
                    if not isinstance(s, int) or s >= 3:
                        pe.wait_ge(t_turn_ready, s - 2)
                    for t, (f0, fr) in enumerate(FT):
                        mm = pe.transpose(ps[0:fr, 5 - par, t * 128:(t + 1) * 128], t_hid[:, 1 - par, f0:f0 + fr],
                                          idn[:])
                    mm.then_inc(t_turned, 1)

            tiles(pe, pe_tile, lag=2)


_OUT = (B, NQ, D)


def kernel(x, ctx_512, g_xattn, g_ffn, L0_xattn_Wq, L0_xattn_Wkv, L0_xattn_Wo, L0_ffn_wqkv, L0_ffn_w1, L0_ffn_w2):
    import concourse.bacc as _bacc
    from concourse.bass_utils import run_bass_kernel_spmd as _run

    def turned(a, *axes):
        return np.ascontiguousarray(np.transpose(a, axes or None))

    order = np.arange(D).reshape(NP, 2, HD).transpose(1, 2, 0).reshape(D)
    num = np.zeros((128, 4, 128), np.float32)
    den = np.zeros((128, 4, 128), np.float32)
    for h in range(H):
        hp, u = h // 2, h % 2
        for d in range(HD):
            num[32 * (hp % 4) + HD * u + d, 2 * (hp // 4) + u, HD * h + d] = 1
            den[32 * (hp % 4) + 16 + HD * u + d, 2 * (hp // 4) + u, HD * h + d] = 1
    mask = np.zeros((D, H), mybir.dt.np(BF16) if hasattr(mybir.dt, "np") else np.float32)
    for p, channel in enumerate(order):
        mask[p, channel // HD] = 1
    pack = {name: np.zeros((128, z - a), np.float32) for name, (a, z) in PACK.items()}
    part, pair = np.arange(128), np.arange(2 * 128)
    cols = np.arange(B * E + E)
    sums = (pair[:, None] // E < cols // E) & (pair[:, None] % E == cols % E)
    pack["batches"][:] = sums.reshape(2, 128, -1).transpose(1, 0, 2).reshape(128, -1)
    pack["before"][:] = part[:, None] < part
    pack["ones"][:] = 1
    pack["region"][:] = REGION * np.arange(E)
    pack["fill"][:] = REGION * np.arange(E) + part[:, None]
    pack["spare"][:] = 2 * TOK + 128 * np.arange(E + SPARE) + part[:, None]
    pack["token"][:NQ] = (np.arange(2 * B) * NQ + part[:NQ, None])
    pack["rows"][:] = 128 * np.arange(TILES)
    pack["full"][:] = np.tile(128 * np.arange(FULL), E)
    pack["upto"][:] = np.tril(np.ones((E, E))).reshape(-1)
    x, wkv = np.asarray(x), np.asarray(L0_xattn_Wkv)
    arrays = {
        "x": np.ascontiguousarray(x),
        "ctx_t": turned(np.asarray(ctx_512), 0, 2, 1),
        "g_x": np.asarray(g_xattn), "g_f": np.asarray(g_ffn),
        "wq_t": turned(np.asarray(L0_xattn_Wq)[order]),
        "wk_t": turned(wkv[:D][order]),
        "wv_t": turned(wkv[D:]),
        "wo_t": turned(np.asarray(L0_xattn_Wo)),
        "wr_t": turned(np.asarray(L0_ffn_wqkv)),
        "w1_t": turned(np.asarray(L0_ffn_w1), 2, 0, 1).reshape(D, E * 2 * F),
        "w2_t": turned(np.asarray(L0_ffn_w2), 0, 2, 1),
        "ident": np.eye(128, dtype=np.float32),
        "head_mask": mask,
        "pick_num": num,
        "pick_den": den,
        "rank": np.tile(np.arange(E, 0, -1, dtype=np.float32), (NQ, 1)),
        "pack": np.concatenate(list(pack.values()), axis=1),
    }
    nc = _bacc.Bacc("TRN2", target_bir_lowering=False, num_devices=1)
    args = [nc.dram_tensor(f"in_{k}", a.shape, mybir.dt.from_np(a.dtype), kind="ExternalInput").ap()
            for k, a in arrays.items()]
    args.append(nc.dram_tensor("out", _OUT, F32, kind="ExternalOutput").ap())
    build(nc, *args)
    r = _run(nc, [{f"in_{k}": a for k, a in arrays.items()}], core_ids=[0])
    return r.results[0]["out"]
```

```python
from contextlib import ExitStack

import numpy as np

import concourse.bass as bass
from concourse import mybir

F32 = mybir.dt.float32
I32 = mybir.dt.int32
U32 = mybir.dt.uint32
BF16 = mybir.dt.bfloat16
ALU = mybir.AluOpType
ACT = mybir.ActivationFunctionType
AX = mybir.AxisListType

B, NQ, D = 32, 100, 128
NK, L = 1444, 64
H, HD = 16, 8
NP = H // 2
E, F = 8, 352
EPS = 1e-5
SCALE = HD ** -0.5
LOWEST = -3.0e38

KT = -(-NK // 128)
ROWS = H * NQ
RT = -(-ROWS // 128)
CH = [482, 482, 480]
CO = [0, 482, 964]
NC = len(CH)
SM = RT * NC
UNITS = 2 * KT
HW = ROWS // 2
PW = 2 * NQ
KPART = [0, 0, 0, 1, 1, 2]
QPART = [0, 1, 2, 0, 1, 0]
UROWS = len(KPART) * HD
KROWS = 2 * UROWS + 2
CB = 4
CT = CB * NQ
NCH = B // CB
FT = [(0, 128), (128, 128), (256, 96)]
TOK = B * NQ
LN_STEPS, RT_STEPS = 9, 26
REGION = TOK + 256
TILES = -(-2 * TOK // 128) + E - 1
SPARE = E
PEEL = 4
SLOTS = 4
assert (TILES - 1 - PEEL) % SLOTS == 0
ROW = D + 2
DMA = 16
COPIES = 2 * len(KPART)

AHEAD = 13
PLAN = [[] for _ in range(UNITS)]
for _u, _use in ((3, ("o", -1, 0)), (5, ("k", 2, 0)), (6, ("y", -1, 0)), (8, ("k", 2, 1)), (10, ("k", 2, 2)),
                 (12, ("v", 1, 0)), (14, ("v", 1, 1)), (16, ("c", -2, 0)), (18, ("m", 1, 0)), (20, ("v", 1, 2)),
                 (21, ("n", -1, 0)), (22, ("r", -1, 0))):
    PLAN[_u].append(_use)
_n = AHEAD
for _u in range(UNITS):
    _take = range(_n, _n + 2 - sum(_use[0] not in "nrc" for _use in PLAN[_u]))
    PLAN[_u] = [("s", 1, m) if m < SM else ("t", 2, m - SM) for m in _take] + PLAN[_u]
    _n = _take.stop
assert _n == SM + AHEAD
FIRST = [("k", 0, n) for n in range(NC)] + [("s", 0, n) for n in range(SM)] + [("k", 1, n) for n in range(NC)] \
    + [("m", 0, 0)] + [("s", 1, n) for n in range(4)] + [("v", 0, n) for n in range(NC)] \
    + [("s", 1, n) for n in range(4, AHEAD)]
ALL = "skvmoytnrc"
STEPS = [[] for _ in range(UNITS)]
for _u, _steps in ((1, "r1"), (2, "r2"), (3, "r3"), (5, "r4 r5"), (6, "r6 r7"), (7, "n1 r8"),
                   (8, "n2 r9 r10"), (9, "r11"), (10, "n3 r12 r13"), (11, "n4"), (12, "n5 r14 r15"), (13, "n6 r16"),
                   (14, "r17 r18 r19"), (16, "n7"), (17, "n8"), (18, "n9"), (19, "r20"), (20, "n10 r21"),
                   (21, "r22 r23"), (22, "r24 r25 r26"), (23, "r27 r28 r29 r30 r31")):
    STEPS[_u] = [(_step[0], int(_step[1:])) for _step in _steps.split()]
NORM, ROUTE_1, ROUTE_2 = range(1, 11), range(1, 20), range(20, 32)
TAIL = [("o", B - 1), ("c", B - 2), ("y", B - 1), ("n", B - 1), ("r", B - 1), ("c", B - 1)]


def kinds_of(i):
    return "skvmt" if i == 0 else "skvmoytnr" if i == 1 else "svmoynrc" if i == B - 2 else \
        "oynrc" if i == B - 1 else ALL


def uses_of(kinds):
    return [use for units in PLAN for use in units if use[0] in kinds]


PACK, _at = {}, 0
for _name, _cols in (("before", 128), ("ones", 128), ("region", E), ("fill", 2 * E),
                     ("spare", E + SPARE), ("token", 2 * B), ("rows", TILES), ("full", E * (TOK // 128 + 1)),
                     ("upto", E * E), ("root", 1)):
    PACK[_name] = (_at, _at + _cols)
    _at += _cols
PACKED = _at
FULL = TOK // 128 + 1


def key_rows(t):
    return min(128, NK - 128 * t)


def score_rows(t):
    return min(128, ROWS - 128 * t)


def build(nc, x, ctx_t, g_x, g_f, wq_t, wk_t, wv_t, wo_t, wr_t, w1_t, w2_t,
          ident, head_mask, pick_num, pick_den, rank, pack, out):
    with ExitStack() as stack:
        def sb(name, shape, dt=F32):
            return stack.enter_context(nc.sbuf_tensor(name, shape, dt))

        def sem(name):
            return stack.enter_context(nc.semaphore(name))

        xs = sb("xs", [NQ, B * D])
        q_part = sb("q_part", [128, 3, B * NQ], BF16)
        ctx = sb("ctx", [L, 2, NK])
        k_full = sb("k_full", [128, NK])
        k_rest = sb("k_rest", [128, NK])
        k_hi = sb("k_hi", [128, 2, NK], BF16)
        k_mid = sb("k_mid", [128, NK], BF16)
        k_lo = sb("k_lo", [128, NK], BF16)
        k_stack = sb("k_stack", [128, 2, NP, NK], BF16)
        q_full = sb("q_full", [128, 2, CT])
        q_rest = sb("q_rest", [128, 2, CT])
        q_stack = sb("q_stack", [KROWS, 2, RT * 128], BF16)
        v_ones = sb("v_ones", [128, 2, KT, NP, 32])
        probs = sb("probs", [128, 4, HW])
        q_block = sb("q_block", [128, 2, H, NQ], BF16)
        maxes = sb("maxes", [128, 2, RT, NC])
        neg_max = sb("neg_max", [128, RT])
        max_row = sb("max_row", [RT, 2, 128], BF16)
        o_sum = sb("o_sum", [128, 4 * NQ])
        den_inv = sb("den_inv", [128, NQ])
        o_norm = sb("o_norm", [128, NQ])
        xn = sb("xn", [NQ, 2, CT * D // NQ])
        wq = sb("wq", [D, D])
        wk = sb("wk", [L, D])
        wv = sb("wv", [L, D])
        wo = sb("wo", [D, D])
        wr = sb("wr", [D, 3 * E])
        idn = sb("idn", [128, 128])
        hmask = sb("hmask", [128, H], BF16)
        pnum = sb("pnum", [128, 4, 128])
        pden = sb("pden", [128, 4, 128])
        rnk = sb("rnk", [NQ, E])
        g_in = sb("g_in", [NQ, 2])
        g_tanh = sb("g_tanh", [NQ, 2])
        stats = sb("stats", [NQ, B * 6])
        mean = sb("mean", [NQ, B])
        rstd = sb("rstd", [NQ, B])
        tmp = sb("tmp", [NQ, 4, B])
        packed = sb("packed", [128, PACKED])
        choice = sb("choice", [NQ, 2, 2, ROW])
        ln = sb("ln", [NQ, 8])
        x_turned = sb("x_turned", [D, NQ])
        mixed = sb("mixed", [NQ, 3 * E])
        outer = sb("outer", [NQ, 3, E * E])
        route = sb("route", [NQ, 8, E])
        pick = sb("pick", [NQ, 8])
        count = sb("count", [NQ, E])
        spots = sb("spots", [128, 2 * E])
        run = sb("run", [128, E])
        place = sb("place", [NQ, 2, 2], U32)
        fill_place = sb("fill_place", [128, 2 * E], U32)
        table = sb("table", [1, 2, TILES], I32)
        t_gate = sb("t_gate", [128, SLOTS])
        t_dest = sb("t_dest", [128, SLOTS], U32)

        rows_d = nc.dram_tensor("sorted_rows", [E * REGION + SPARE * 128, ROW], F32).ap()
        y_d = nc.dram_tensor("expert_out", [2 * TOK + (E + SPARE) * 128, D], F32).ap()

        xt = probs[:].rearrange("p a b -> p (a b)")
        k_flat = k_stack[:].rearrange("p a b n -> p (a b n)").bitcast(F32)
        w1 = k_flat[:, 0:E * 2 * F]
        half = NP * NK // 2
        assert E * 2 * F <= half
        w2 = k_flat[:, half:half + E * len(FT) * D].rearrange("p (e t d) -> p e t d", e=E, t=len(FT))
        v_flat = v_ones[:].rearrange("p a b c d -> p (a b c d)")
        w_end = half + E * len(FT) * D
        zeros = k_flat[:, w_end:w_end + (E + SPARE) * ROW].rearrange("p (t r) -> p t r", r=ROW)
        y_in = [k_flat[0:NQ, n * B * D:(n + 1) * B * D] for n in (0, 1)]

        def const(name, rows=128):
            return packed[0:rows, PACK[name][0]:PACK[name][1]]

        past_end = k_rest[0:1, 776:776 + TILES * E].rearrange("q (s e) -> q s e", e=E)
        q_flat = q_full[:].rearrange("p a n -> p (a n)")
        is_full = q_flat[0:1, 0:E * FULL].rearrange("q (e j) -> q e j", e=E)
        partial = q_flat[0:1, 224:224 + E * E].rearrange("q (e j) -> q e j", e=E)
        e_tiles, e_end, e_jump = (q_flat[0:1, 288 + n * E:288 + (n + 1) * E] for n in range(3))
        jumped, row_of, expert_of = (q_flat[0:1, 320 + n * TILES:320 + (n + 1) * TILES] for n in range(3))
        past_jump = q_rest[:].rearrange("p a n -> p (a n)")[0:1, 0:TILES * E].rearrange("q (s e) -> q s e", e=E)
        room = [0]

        def take(cols, n):
            room[0] += cols * n
            return v_flat[:, room[0] - cols * n:room[0]].rearrange("p (n c) -> p n c", n=n)

        t_row, t_x, t_silu = take(ROW, SLOTS), take(128, 2), take(F, 2)
        t_hid, t_turn, t_y = take(F, 2), take(3 * 128, 2), take(D, SLOTS)

        ps = stack.enter_context(nc.psum_tensor("ps", [128, 8, 512], F32))
        RING, OB = 4, 7

        x_in = [sem(f"x_in{n}") for n in range(4)]
        first_in = sem("first_in")
        const_in = sem("const_in")
        w_in = sem("w_in")
        ctx_in = [sem("ctx_in0"), sem("ctx_in1")]
        k_in = sem("k_in")
        q_in = sem("q_in")
        max_in = sem("max_in")
        cleared = sem("cleared")
        v_step = sem("v_step")
        a_step = sem("a_step")
        v_asks = sem("v_asks")
        tanh_done = sem("tanh_done")
        stats_ready = sem("stats_ready")
        xn_ready = sem("xn_ready")
        xn_turned = sem("xn_turned")
        xt_ready = sem("xt_ready")
        q_made = sem("q_made")
        q_scaled = sem("q_scaled")
        q_split = sem("q_split")
        k_made = sem("k_made")
        k_taken = sem("k_taken")
        k_parted = sem("k_parted")
        v_made = sem("v_made")
        v_taken = sem("v_taken")
        block_ready = sem("block_ready")
        sm_made = sem("sm_made")
        sm_taken = sem("sm_taken")
        neg_ready = sem("neg_ready")
        max_turned = sem("max_turned")
        row_ready = sem("row_ready")
        st_made = sem("st_made")
        exp_done = sem("exp_done")
        pv_done = sem("pv_done")
        o_copied = sem("o_copied")
        nd_made = sem("nd_made")
        inv_ready = sem("inv_ready")
        on_ready = sem("on_ready")
        y_made = sem("y_made")
        y_added = sem("y_added")
        var_ready = sem("var_ready")
        ln_step = sem("ln_step")
        root_ready = sem("root_ready")
        norm_ready = sem("norm_ready")
        x2_turned = sem("x2_turned")
        x2_ready = sem("x2_ready")
        mixed_made = sem("mixed_made")
        mixed_ready = sem("mixed_ready")
        rt_step = sem("rt_step")
        less_ready = sem("less_ready")
        exp_ready = sem("exp_ready")
        counted = sem("counted")
        diff_ready = sem("diff_ready")
        ratio_ready = sem("ratio_ready")
        spots_made = sem("spots_made")
        spots_ready = sem("spots_ready")
        places_ready = sem("places_ready")
        rows_out = [sem("rows_out0"), sem("rows_out1")]
        zeros_ready = sem("zeros_ready")
        spare_out = sem("spare_out")
        fill_ready = sem("fill_ready")
        fill_out = sem("fill_out")
        table_ready = sem("table_ready")
        t_row_in = [sem(f"t_row_in{n}") for n in range(SLOTS)]
        t_x_turned = sem("t_x_turned")
        t_x_ready = sem("t_x_ready")
        t_dest_ready = sem("t_dest_ready")
        t_h_made = sem("t_h_made")
        t_silu_done = sem("t_silu_done")
        t_hid_ready = sem("t_hid_ready")
        t_turned = sem("t_turned")
        t_turn_ready = sem("t_turn_ready")
        t_y_made = sem("t_y_made")
        t_y_ready = sem("t_y_ready")
        t_y_out = [sem(f"t_y_out{n}") for n in range(SLOTS)]
        y_back = [sem(f"y_back{n}") for n in range(NCH)]
        added = sem("added")
        out_done = sem("out_done")

        block = stack.enter_context(nc.Block())

        def ring_read(eng, kind, b, n):
            if kind in "st":
                eng.wait_ge(sm_taken, b * SM + n + 1)
            elif kind == "k":
                eng.wait_ge(k_taken, b * NC + n + 1)
            elif kind == "v":
                eng.wait_ge(v_taken, b * NC + n + 1)
            elif kind == "m":
                eng.wait_ge(row_ready, b * 2 + 2)
            elif kind == "o":
                eng.wait_ge(on_ready, b + 1)
            elif kind == "y":
                eng.wait_ge(y_added, b + 1)
            elif kind == "n":
                eng.wait_ge(x2_ready, b + 1)
            elif kind == "r":
                eng.wait_ge(mixed_ready, b + 1)
            else:
                eng.wait_ge(spots_ready, b + 1)

        def batches(eng, body, last=B):
            for i in range(4):
                body(i, i // 2, i % 2, kinds_of(i), kinds_of(i - 1) if i else None)
            with eng.Fori(2, B // 2 - 1) as it:
                for par in (0, 1):
                    body(it * 2 + par, it, par, ALL, ALL)
            for i in (B - 2, B - 1):
                body(i, i // 2, i % 2, kinds_of(i), kinds_of(i - 1))

        def tiles(eng, body, lag=0):
            values = {}
            for s in range(PEEL):
                body(s, s // SLOTS, s % SLOTS, s, values)
            with eng.Fori(0, (TILES - 1 - PEEL) // SLOTS) as it:
                values = {}
                for s in range(PEEL, PEEL + SLOTS):
                    body(it * SLOTS + s, it + s // SLOTS, s % SLOTS, s, values)
            values = {}
            for s in range(TILES - 1, TILES + lag):
                body(s, s // SLOTS, s % SLOTS, s, values)

        @block.sync
        def _(sp):
            step = B // len(x_in)
            for n, done in enumerate(x_in):
                if n == 1:
                    for dst, src in ((wk, wk_t), (idn, ident), (wq, wq_t)):
                        sp.dma_start(dst[:], src).then_inc(first_in, DMA)
                    sp.dma_start(ctx[:, 0, :], ctx_t[0]).then_inc(ctx_in[0], DMA)
                sp.dma_start(xs[:, n * step * D:(n + 1) * step * D].rearrange("q (b d) -> q b d", b=step),
                             x[n * step:(n + 1) * step].rearrange("b q d -> q b d")).then_inc(done, DMA)
            sp.dma_start(ctx[:, 1, :], ctx_t[1]).then_inc(ctx_in[1], DMA)
            for dst, src in ((hmask, head_mask), (wv, wv_t), (wo, wo_t), (wr, wr_t), (rnk, rank),
                             (pnum, pick_num), (pden, pick_den), (packed, pack)):
                sp.dma_start(dst[:], src).then_inc(const_in, DMA)
            for n, g in enumerate((g_x, g_f)):
                sp.dma_start(g_in[:, n:n + 1], g.rearrange("(a b) -> a b", a=1).to_broadcast([NQ, 1])) \
                    .then_inc(const_in, DMA)

            def held(value):
                return value if isinstance(value, int) else sp.snap(sp.to_reg(value))

            def stacks(b, par, parts, tokens):
                sp.wait_ge(k_taken, parts)
                sp.wait_ge(k_parted, parts)
                for s, part in enumerate(KPART):
                    src = (k_hi[:, par, :], k_mid[:], k_lo[:])[part]
                    for u in (0, 1):
                        r = u * UROWS + s * HD
                        sp.dma_start(k_stack[r:r + HD, par, :, :], src[64 * u:64 * u + 64, :]).then_inc(k_in, DMA)
                if isinstance(b, int) and b == 0:
                    sp.wait_ge(q_split, 1)
                for s, part in enumerate(QPART):
                    for u in (0, 1):
                        r = u * UROWS + s * HD
                        dst = q_stack[r:r + HD, par, 0:ROWS].rearrange("p (h n) -> p h n", h=NP)
                        sp.dma_start(dst[:, :, u * NQ:(u + 1) * NQ],
                                     q_part[64 * u:64 * u + 64, part, bass.ds(tokens, NQ)]).then_inc(q_in, DMA)

            def max_rows(par, parts):
                sp.wait_ge(row_ready, parts)
                for n in (0, 1):
                    dst = q_stack[2 * UROWS + n:2 * UROWS + n + 1, par, :].rearrange("p (t n) -> p t n", t=RT)
                    sp.dma_start(dst, max_row[:, n, :]).then_inc(max_in, DMA)

            sp.wait_ge(cleared, 6)
            stacks(0, 0, NC, 0)
            sp.wait_ge(v_made, NC)
            max_rows(0, 2)
            sp.wait_ge(q_split, NCH)

            def body(i, it, par, kinds, before):
                if "s" not in kinds:
                    return
                units, copies, copied = held(i * UNITS), held((i + 1) * (COPIES * DMA)), held((i + 1) * (2 * DMA))
                parts, tokens, turned = held((i + 2) * NC), held((i + 1) * NQ), held((i + 2) * 2)
                if "k" in kinds:
                    src = ctx_t[bass.ds(i + 2, 1)].rearrange("a l k -> (a l) k")
                    sp.dma_start(ctx[:, par, :], src).then_inc(ctx_in[par], DMA)
                if "o" in kinds:
                    sp.wait_ge(st_made, units)
                sp.wait_ge(k_in, copies)
                sp.wait_ge(q_in, copies)
                stacks(i + 1, 1 - par, parts, tokens)
                sp.wait_ge(max_in, copied)
                sp.wait_ge(v_made, parts)
                max_rows(1 - par, turned)

            batches(sp, body)
            sp.wait_ge(st_made, (B - 1) * UNITS)
            sp.dma_start(w1, w1_t).then_inc(w_in, DMA)
            sp.wait_ge(st_made, B * UNITS)
            for t, (f0, fr) in enumerate(FT):
                sp.dma_start(w2[0:fr, :, t, :], w2_t[:, f0:f0 + fr, :].rearrange("e f d -> f e d")).then_inc(w_in, DMA)
            sp.wait_ge(zeros_ready, 2)
            sp.dma_start(rows_d[E * REGION:E * REGION + SPARE * 128].rearrange("(t p) r -> p t r", p=128),
                         zeros[:, E:E + SPARE, :]).then_inc(spare_out, DMA)
            sp.wait_ge(spare_out, DMA)
            sp.wait_ge(fill_out, 2 * E * DMA)
            for par in (0, 1):
                sp.wait_ge(rows_out[par], B // 2 * 2 * DMA)
            sp.wait_ge(table_ready, 2)

            def load_tile(s, turn, slot, step, values):
                row = sp.value_load(table[0:1, 0, bass.ds(s, 1)], min_val=0,
                                    max_val=E * REGION + (SPARE - 1) * 128)
                if not isinstance(s, int) or s >= SLOTS:
                    past = s - (SLOTS - 1)
                    past = past if isinstance(past, int) else held(past)
                    sp.wait_ge(t_x_turned, past)
                    sp.wait_ge(t_dest_ready, past)
                sp.dma_start(t_row[:, slot, :], rows_d[bass.ds(row, 128), :]).then_inc(t_row_in[slot], DMA)

            tiles(sp, load_tile)
            for slot in range(SLOTS):
                sp.wait_ge(t_y_out[slot], len(range(slot, TILES, SLOTS)) * DMA)
            for c in range(NCH):
                for n in (0, 1):
                    sp.dma_start(y_in[n][:, c * CB * D:(c + 1) * CB * D].rearrange("q (b d) -> q b d", b=CB),
                                 y_d[n * TOK + c * CT:n * TOK + (c + 1) * CT].rearrange("(b q) d -> q b d", b=CB)) \
                        .then_inc(y_back[c], DMA)
            for c in range(NCH):
                sp.wait_ge(added, 2 * c + 2)
                sp.dma_start(out[c * CB:(c + 1) * CB].rearrange("b q d -> q b d"),
                             xs[:, c * CB * D:(c + 1) * CB * D].rearrange("q (b d) -> q b d", b=CB)) \
                    .then_inc(out_done, DMA)
            sp.wait_ge(out_done, NCH * DMA)

        @block.gpsimd
        def _(pool):
            pool.memset(q_stack[:], 0.0).then_inc(cleared, 1)
            pool.memset(maxes[:], 0.0).then_inc(cleared, 1)
            pool.memset(v_ones[:, :, :, :, 2 * HD:32], 1.0).then_inc(cleared, 1)
            pool.wait_ge(cleared, 3)
            pool.memset(v_ones[:, :, KT - 1, :, :], 0.0).then_inc(cleared, 1)
            pool.wait_ge(cleared, 4)
            pool.memset(v_ones[0:key_rows(KT - 1), :, KT - 1, :, 2 * HD:32], 1.0).then_inc(cleared, 1)
            pool.memset(k_stack[2 * UROWS:KROWS, :, :, :], 1.0).then_inc(cleared, 1)

            def root(b):
                pool.wait_ge(var_ready, b + 1)
                pool.tensor_tensor(ln[:, 4:5], ln[:, 3:4], const("root", NQ), ALU.pow).then_inc(root_ready, 1)

            def scatter(dst, where, src, done):
                pool.indirect_dma_start(dst, bass.IndirectOffsetOnAxis(ap=where, axis=0), src, None) \
                    .then_inc(done, DMA)

            placed = pool.alloc_register("placed")
            pool.reg_mov(placed, 2 * 3)

            def put_rows(b, par):
                if isinstance(b, int):
                    pool.wait_ge(places_ready, 2 * (b + 1))
                else:
                    pool.wait_ge(places_ready, placed)
                    pool.reg_add(placed, placed, 2)
                for n in (0, 1):
                    scatter(rows_d, place[:, par, n:n + 1], choice[:, par, n, :], rows_out[par])

            def block_q(b, par):
                q = q_part[:, 0, bass.ds(b * NQ, NQ)]
                pool.tensor_tensor(q_block[:, par, :, :], q.unsqueeze(1).to_broadcast([128, H, NQ]),
                                   hmask[:].unsqueeze(2).to_broadcast([128, H, NQ]), ALU.mult).then_inc(block_ready, 1)

            def part_k(b, par):
                pool.wait_ge(k_taken, (b + 1) * NC)
                if not (isinstance(b, int) and b == 0):
                    pool.wait_ge(k_in, b * COPIES * DMA)
                pool.tensor_tensor(k_mid[:], k_full[:], k_hi[:, par, :], ALU.subtract).then_inc(k_parted, 1)
                pool.tensor_tensor(k_rest[:], k_full[:], k_hi[:, par, :], ALU.subtract).then_inc(k_parted, 1)
                pool.wait_ge(k_parted, b * 3 + 2)
                pool.tensor_tensor(k_lo[:], k_rest[:], k_mid[:], ALU.subtract).then_inc(k_parted, 1)

            pool.wait_ge(const_in, DMA * 10)
            pool.wait_ge(cleared, 6)
            part_k(0, 0)
            pool.wait_ge(q_scaled, 1)
            block_q(0, 0)
            block_q(1, 1)
            part_k(1, 1)
            pool.wait_ge(q_scaled, NCH)

            def body(i, it, par, kinds, before):
                if "k" in kinds:
                    pool.wait_ge(sm_made, (i + 1) * SM)
                    block_q(i + 2, par)
                if "n" in kinds:
                    root(i - 1)
                if "k" in kinds:
                    part_k(i + 2, par)
                if "c" in kinds:
                    put_rows(i - 2, par)

            batches(pool, body)

            pool.wait_ge(st_made, B * UNITS)
            pool.memset(zeros, 0.0).then_inc(zeros_ready, 1)
            pool.wait_ge(zeros_ready, 1)
            pool.tensor_copy(zeros[:, :, D + 1], const("spare")).then_inc(zeros_ready, 1)
            put_rows(B - 2, 0)
            pool.wait_ge(zeros_ready, 2)
            pool.wait_ge(fill_ready, 1)
            for n in range(2 * E):
                if n == 2:
                    root(B - 1)
                scatter(rows_d, fill_place[:, n:n + 1], zeros[:, n % E, :], fill_out)
            pool.wait_ge(fill_out, 2 * E * DMA)
            put_rows(B - 1, 1)

            put = pool.alloc_register("put")
            pool.reg_mov(put, PEEL + 1)

            def put_tile(s, turn, slot, step, values):
                if isinstance(s, int):
                    pool.wait_ge(t_y_ready, s + 1)
                else:
                    pool.wait_ge(t_y_ready, put)
                    pool.reg_add(put, put, 1)
                scatter(y_d, t_dest[:, slot:slot + 1], t_y[:, slot, :], t_y_out[slot])

            tiles(pool, put_tile)

        @block.scalar
        def _(act):
            def root():
                act.wait_ge(v_asks, 1)
                act.activation(tmp[:, 3, :], tmp[:, 2, :], ACT.Sqrt).then_inc(a_step, 1)

            def take_xt(c):
                act.wait_ge(xn_turned, c + 1)
                act.activation(xt[:, c * CT:(c + 1) * CT], ps[:, c % 2, 0:CT], ACT.Copy).then_inc(xt_ready, 1)

            def take_first(uses):
                for n_use, (kind, b, n) in enumerate(uses):
                    if kind == "k":
                        take_k(b, 0, b % 2, n, RING + n_use % 3)
                    elif kind == "v":
                        take_v(b, b % 2, n, RING + n_use % 3)

            def take_q(c):
                if c >= 2:
                    act.wait_ge(q_split, c - 1)
                act.wait_ge(q_made, c + 1)
                src = ps[:, 2 + c % 2, 0:CT]
                act.activation(q_full[:, c % 2, :], src, ACT.Copy, scale=SCALE)
                act.activation(q_part[:, 0, c * CT:(c + 1) * CT], src, ACT.Copy, scale=SCALE).then_inc(q_scaled, 1)

            def take_k(b, it, par, n, bank):
                act.wait_ge(k_made, b * NC + n + 1)
                if n == 0 and not isinstance(b, int) or n == 0 and b >= 1:
                    act.wait_ge(k_parted, b * 3)
                if n == 0 and (not isinstance(b, int) or b >= 2):
                    act.wait_ge(sm_made, (b - 1) * SM)
                    act.wait_ge(k_in, (b - 1) * COPIES * DMA)
                src = ps[:, bank, 0:CH[n]]
                act.activation(k_full[:, CO[n]:CO[n] + CH[n]], src, ACT.Copy)
                act.activation(k_hi[:, par, CO[n]:CO[n] + CH[n]], src, ACT.Copy).then_inc(k_taken, 1)

            def take_v(b, par, n, bank):
                act.wait_ge(v_made, b * NC + n + 1)
                if n == 0 and (not isinstance(b, int) or b >= 2):
                    act.wait_ge(pv_done, (b - 1) * UNITS)
                full = sum(key_rows(t) == 128 for t in range(4 * n, 4 * n + 4))
                src = ps[:, bank, :].rearrange("p (t h c) -> p t h c", t=4, h=NP)
                dst = v_ones[:, par, 4 * n:4 * n + 4, :, 0:2 * HD]
                last = act.activation(dst[:, 0:full], src[:, 0:full], ACT.Copy)
                if full < 4:
                    r = key_rows(KT - 1)
                    last = act.activation(dst[0:r, full], src[0:r, full], ACT.Copy)
                last.then_inc(v_taken, 1)

            take_first(FIRST[:NC])
            root()
            for c in range(NCH):
                take_xt(c)
                if c >= 1:
                    take_q(c - 1)
            take_q(NCH - 1)
            act.wait_ge(const_in, DMA * 10)
            act.activation(g_tanh[:], g_in[:], ACT.Tanh).then_inc(tanh_done, 1)
            act.wait_ge(cleared, 6)
            take_first([("", 0, 0)] * NC + FIRST[NC:])
            used = [len(FIRST)]

            def copy_o(b, last=False):
                act.wait_ge(pv_done, (b + 1) * UNITS)
                if not isinstance(b, int) or b >= 1:
                    act.wait_ge(nd_made, b)
                act.activation(o_sum[:], ps[:, OB, 0:4 * NQ], ACT.Copy).then_inc(o_copied, 1)

            def take_turned(b, bank):
                act.wait_ge(x2_turned, b + 1)
                if not isinstance(b, int) or b >= 1:
                    act.wait_ge(mixed_made, b)
                act.activation(x_turned[:], ps[:, bank, 0:NQ], ACT.Copy).then_inc(x2_ready, 1)

            def take_mixed(b, bank):
                act.wait_ge(mixed_made, b + 1)
                if not isinstance(b, int) or b >= 1:
                    act.wait_ge(counted, b)
                act.activation(mixed[:], ps[0:NQ, bank, 0:3 * E], ACT.Copy).then_inc(mixed_ready, 1)

            def take_spots(b, bank):
                act.wait_ge(spots_made, b + 1)
                act.activation(spots[:], ps[:, bank, 0:2 * E], ACT.Copy).then_inc(spots_ready, 1)

            def exp_products(b):
                act.wait_ge(less_ready, b + 1)
                act.activation(outer[:, 1, :], outer[:, 0, :], ACT.Exp).then_inc(exp_ready, 1)

            def exp_ratio(b):
                act.wait_ge(diff_ready, b + 1)
                act.activation(pick[:, 3:4], pick[:, 2:3], ACT.Exp).then_inc(ratio_ready, 1)

            def body(i, it, par, kinds, before):
                for u in range(UNITS):
                    act.wait_ge(st_made, i * UNITS + u + 1)
                    if not isinstance(i, int) or i * UNITS + u >= 4:
                        act.wait_ge(pv_done, i * UNITS + u - 3)
                    r = key_rows(u // 2)
                    act.activation(probs[0:r, u % 4, :].rearrange("p (a n) -> p a n", a=2),
                                   ps[0:r, 2 * (u % 2):2 * (u % 2) + 2, 0:CT], ACT.Exp).then_inc(exp_done, 1)
                    if u == 1 and "o" in kinds:
                        copy_o(i - 1)
                    for kind, off, n in PLAN[u]:
                        if kind in kinds:
                            bank = RING + used[0] % 3
                            used[0] += 1
                            if kind == "k":
                                take_k(i + off, it, par, n, bank)
                            elif kind == "v":
                                take_v(i + off, 1 - par, n, bank)
                            elif kind == "n":
                                take_turned(i - 1, bank)
                            elif kind == "r":
                                take_mixed(i - 1, bank)
                            elif kind == "c":
                                take_spots(i - 2, bank)
                    if u == 4 and "c" in kinds:
                        exp_products(i - 2)
                    if u == 17 and "c" in kinds:
                        exp_ratio(i - 2)

            batches(act, body)
            exp_products(B - 2)
            copy_o(B - 1)
            exp_ratio(B - 2)
            for n_use, (kind, b) in enumerate(TAIL):
                bank = RING + (used[0] + n_use) % 3
                if kind == "n":
                    take_turned(b, bank)
                elif kind == "r":
                    take_mixed(b, bank)
                    exp_products(b)
                    exp_ratio(b)
                elif kind == "c":
                    take_spots(b, bank)

            def take_x(s):
                act.wait_ge(t_x_turned, s + 1)
                if not isinstance(s, int) or s >= 2:
                    act.wait_ge(t_h_made, s - 1)
                par = carried["slot"] % 2
                act.activation(t_x[:, par, :], ps[:, 6, 0:128], ACT.Copy).then_inc(t_x_ready, 1)

            carried = {}

            def act_tile(s, turn, slot, step, values):
                par = slot % 2
                if isinstance(s, int) and s == 0:
                    carried["slot"] = 0
                    take_x(0)
                if not isinstance(s, int) or s + 1 < TILES:
                    carried["slot"] = slot + 1
                    take_x(s + 1)
                if not isinstance(s, int) or s < TILES:
                    act.wait_ge(t_h_made, s + 1)
                    if not isinstance(s, int) or s >= 2:
                        act.wait_ge(t_hid_ready, s - 1)
                    act.activation(t_silu[:, par, :], ps[:, 2 * par, 0:F], ACT.Silu).then_inc(t_silu_done, 1)
                if not isinstance(s, int) or s >= 1:
                    act.wait_ge(t_turned, s)
                    if not isinstance(s, int) or s >= 3:
                        act.wait_ge(t_y_made, s - 2)
                    act.activation(t_turn[:, 1 - par, 0:256], ps[:, 5 - par, 0:256], ACT.Copy)
                    fr = FT[2][1]
                    act.activation(t_turn[0:fr, 1 - par, 256:384], ps[0:fr, 5 - par, 256:384], ACT.Copy) \
                        .then_inc(t_turn_ready, 1)

            tiles(act, act_tile, lag=1)

        @block.vector
        def _(dve):
            steps = [0]

            def step(ins):
                ins.then_inc(v_step, 1)
                steps[0] += 1
                dve.wait_ge(v_step, steps[0])

            def norm():
                dve.wait_ge(stats_ready, B)
                st = stats[:].rearrange("q (b s) -> q s b", s=6)
                step(dve.tensor_tensor(tmp[:, 0, :], st[:, 1, :], st[:, 4, :], ALU.add))
                step(dve.tensor_scalar(mean[:], tmp[:, 0, :], 0.5, None, ALU.mult))
                step(dve.tensor_tensor(tmp[:, 1, :], st[:, 1, :], st[:, 4, :], ALU.subtract))
                step(dve.tensor_tensor(tmp[:, 0, :], tmp[:, 1, :], tmp[:, 1, :], ALU.mult))
                step(dve.scalar_tensor_tensor(tmp[:, 1, :], tmp[:, 0, :], D / 4, st[:, 2, :], ALU.mult, ALU.add))
                step(dve.tensor_tensor(tmp[:, 0, :], tmp[:, 1, :], st[:, 5, :], ALU.add))
                dve.tensor_scalar(tmp[:, 2, :], tmp[:, 0, :], 1.0 / D, EPS, ALU.mult, ALU.add).then_inc(v_asks, 1)
                dve.wait_ge(a_step, 1)
                step(dve.reciprocal(tmp[:, 0, :], tmp[:, 3, :]))
                step(dve.tensor_tensor(tmp[:, 1, :], tmp[:, 0, :], tmp[:, 0, :], ALU.mult))
                step(dve.tensor_tensor(tmp[:, 3, :], tmp[:, 1, :], tmp[:, 2, :], ALU.mult))
                step(dve.tensor_scalar(tmp[:, 1, :], tmp[:, 3, :], -0.5, 1.5, ALU.mult, ALU.add))
                step(dve.tensor_tensor(rstd[:], tmp[:, 0, :], tmp[:, 1, :], ALU.mult))

            def norm_chunk(c):
                if c >= 2:
                    dve.wait_ge(xn_turned, c - 1)
                for t in range(CB):
                    b = c * CB + t
                    ins = dve.tensor_scalar(xn[:, c % 2, t * D:(t + 1) * D], xs[:, b * D:(b + 1) * D],
                                            mean[:, b:b + 1], rstd[:, b:b + 1], ALU.subtract, ALU.mult)
                ins.then_inc(xn_ready, 1)

            def split_q(c):
                of = slice(c * CT, (c + 1) * CT)
                dve.wait_ge(q_scaled, c + 1)
                full, rest = q_full[:, c % 2, :], q_rest[:, c % 2, :]
                step(dve.tensor_tensor(rest, full, q_part[:, 0, of], ALU.subtract))
                step(dve.tensor_copy(q_part[:, 1, of], rest))
                dve.tensor_tensor(q_part[:, 2, of], rest, q_part[:, 1, of], ALU.subtract).then_inc(q_split, 1)

            def statistics(b):
                dve.bn_stats(stats[:, bass.ds(b * 6, 6)], xs[:, bass.ds(b * D, D)]).then_inc(stats_ready, 1)

            for n, done in enumerate(x_in):
                dve.wait_ge(done, DMA)
                for b in range(n * B // 4, (n + 1) * B // 4):
                    statistics(b)
            norm()
            for c in range(NCH):
                norm_chunk(c)
                if c >= 2:
                    split_q(c - 2)
            split_q(NCH - 2)
            split_q(NCH - 1)

            def take_max(b, par, n, bank):
                t, c = n // NC, n % NC
                r = score_rows(t)
                dve.wait_ge(sm_made, b * SM + n + 1)
                if n == 0 and (not isinstance(b, int) or b >= 2):
                    dve.wait_ge(neg_ready, b - 1)
                dve.tensor_reduce(maxes[0:r, par, t, c:c + 1], ps[0:r, bank, 0:CH[c]], AX.X, ALU.max) \
                    .then_inc(sm_taken, 1)

            def join_max(b, par):
                dve.wait_ge(sm_taken, b * SM + SM)
                if not isinstance(b, int) or b >= 1:
                    dve.wait_ge(row_ready, b * 2)
                dve.tensor_reduce(neg_max[:], maxes[:, par, :, :], AX.X, ALU.max, negate=True).then_inc(neg_ready, 1)

            def part_max(b, bank):
                dve.wait_ge(max_turned, b + 1)
                if not isinstance(b, int) or b >= 1:
                    dve.wait_ge(max_in, b * 2 * DMA)
                dve.tensor_copy(max_row[:, 0, :], ps[0:RT, bank, 0:128]).then_inc(row_ready, 1)
                dve.wait_ge(row_ready, b * 2 + 1)
                dve.tensor_tensor(max_row[:, 1, :], ps[0:RT, bank, 0:128], max_row[:, 0, :], ALU.subtract) \
                    .then_inc(row_ready, 1)

            def divide(b, bank):
                dve.wait_ge(nd_made, b + 1)
                dve.reciprocal(den_inv[:], ps[:, bank, 0:NQ]).then_inc(inv_ready, 1)
                dve.wait_ge(inv_ready, b + 1)
                if not isinstance(b, int) or b >= 1:
                    dve.wait_ge(y_made, b)
                dve.tensor_tensor(o_norm[:], ps[:, bank, 128:128 + NQ], den_inv[:], ALU.mult).then_inc(on_ready, 1)

            def add_y(b, bank):
                dve.wait_ge(y_made, b + 1)
                row = xs[:, bass.ds(b * D, D)]
                dve.scalar_tensor_tensor(row, ps[0:NQ, bank, 0:D], g_tanh[:, 0:1], row, ALU.mult, ALU.add) \
                    .then_inc(y_added, 1)

            cube = [outer[:, n, :].rearrange("q (i j) -> q i j", i=E) for n in range(3)]
            wide = [NQ, E, E]

            def second_norm(b, turn, par, n):
                if n in (3, 4, 5, 6, 8, 9, 10):
                    dve.wait_ge(ln_step, b * LN_STEPS + {3: 2, 4: 4, 5: 5, 6: 6, 8: 7, 9: 8, 10: 9}[n])
                if n == 1:
                    dve.wait_ge(y_added, b + 1)
                    statistics(b)
                _, mean0, m2_0, _, mean1, m2_1 = (stats[:, bass.ds(b * 6 + m, 1)] for m in range(6))
                if n == 2:
                    dve.wait_ge(stats_ready, B + b + 1)
                    if not isinstance(b, int) or b >= 1:
                        dve.wait_ge(norm_ready, b)
                    dve.tensor_tensor(ln[:, 0:1], mean0, mean1, ALU.add).then_inc(ln_step, 1)
                    dve.tensor_tensor(ln[:, 2:3], mean0, mean1, ALU.subtract).then_inc(ln_step, 1)
                elif n == 3:
                    dve.tensor_scalar(ln[:, 1:2], ln[:, 0:1], 0.5, None, ALU.mult).then_inc(ln_step, 1)
                    dve.tensor_tensor(ln[:, 5:6], ln[:, 2:3], ln[:, 2:3], ALU.mult).then_inc(ln_step, 1)
                elif n == 4:
                    dve.scalar_tensor_tensor(ln[:, 6:7], ln[:, 5:6], D / 4, m2_0, ALU.mult, ALU.add) \
                        .then_inc(ln_step, 1)
                elif n == 5:
                    dve.tensor_tensor(ln[:, 7:8], ln[:, 6:7], m2_1, ALU.add).then_inc(ln_step, 1)
                elif n == 6:
                    dve.tensor_scalar(ln[:, 3:4], ln[:, 7:8], 1.0 / D, EPS, ALU.mult, ALU.add).then_inc(var_ready, 1)
                elif n == 7:
                    dve.wait_ge(root_ready, b + 1)
                    dve.scalar_tensor_tensor(ln[:, 5:6], ln[:, 4:5], ln[:, 3:4], ln[:, 4:5], ALU.mult, ALU.mult) \
                        .then_inc(ln_step, 1)
                elif n == 8:
                    dve.tensor_scalar(ln[:, 6:7], ln[:, 5:6], -0.5, 1.5, ALU.mult, ALU.add).then_inc(ln_step, 1)
                elif n == 9:
                    dve.tensor_tensor(ln[:, 7:8], ln[:, 4:5], ln[:, 6:7], ALU.mult).then_inc(ln_step, 1)
                elif n == 10:
                    if not isinstance(b, int) or b >= 2:
                        dve.wait_ge(rows_out[par], turn * (2 * DMA))
                    for m in (0, 1):
                        dve.tensor_scalar(choice[:, par, m, 0:D], xs[:, bass.ds(b * D, D)], ln[:, 1:2], ln[:, 7:8],
                                          ALU.subtract, ALU.mult)
                    dve.tensor_copy(choice[:, par, :, D + 1], packed[0:NQ, bass.ds(b * 2 + PACK["token"][0], 2)]) \
                        .then_inc(norm_ready, 1)

            def routing(b, par, n):
                def done(ins):
                    ins.then_inc(rt_step, 1)

                def after(steps):
                    dve.wait_ge(rt_step, b * RT_STEPS + steps)

                def best(k, values, chosen, top):
                    if k == 0:
                        done(dve.tensor_reduce(top, values, AX.X, ALU.max))
                    elif k == 1:
                        done(dve.scalar_tensor_tensor(route[:, 4, :], values, top, rnk[:], ALU.is_equal, ALU.mult))
                    elif k == 2:
                        done(dve.tensor_reduce(pick[:, 4:5], route[:, 4, :], AX.X, ALU.max))
                    else:
                        done(dve.tensor_scalar(chosen, route[:, 4, :], pick[:, 4:5], None, ALU.is_equal))

                if n == 1:
                    dve.wait_ge(mixed_ready, b + 1)
                    done(dve.tensor_tensor(cube[2], mixed[:, 0:E].unsqueeze(2).to_broadcast(wide),
                                           mixed[:, E:2 * E].unsqueeze(1).to_broadcast(wide), ALU.mult))
                elif n == 2:
                    after(1)
                    done(dve.tensor_reduce(route[:, 0, :], cube[2], AX.X, ALU.max))
                elif n == 3:
                    after(2)
                    dve.tensor_tensor(cube[0], cube[2], route[:, 0, :].unsqueeze(2).to_broadcast(wide),
                                      ALU.subtract).then_inc(less_ready, 1)
                elif n == 4:
                    dve.wait_ge(exp_ready, b + 1)
                    done(dve.tensor_reduce(route[:, 1, :], cube[1], AX.X, ALU.add))
                elif n == 5:
                    done(dve.tensor_tensor(cube[2], cube[1], mixed[:, 2 * E:].unsqueeze(1).to_broadcast(wide),
                                           ALU.mult))
                elif n == 6:
                    after(4)
                    done(dve.tensor_reduce(route[:, 2, :], cube[2], AX.X, ALU.add))
                elif n == 7:
                    done(dve.reciprocal(route[:, 3, :], route[:, 1, :]))
                elif n == 8:
                    after(6)
                    done(dve.tensor_tensor(route[:, 0, :], route[:, 2, :], route[:, 3, :], ALU.mult))
                elif n <= 12:
                    after(n - 2)
                    best(n - 9, route[:, 0, :], route[:, 1, :], pick[:, 0:1])
                elif n == 13:
                    after(11)
                    done(dve.scalar_tensor_tensor(route[:, 3, :], route[:, 1, :], LOWEST, route[:, 0, :],
                                                  ALU.mult, ALU.add))
                elif n <= 17:
                    after(n - 2)
                    best(n - 14, route[:, 3, :], route[:, 2, :], pick[:, 1:2])
                elif n == 18:
                    after(16)
                    dve.tensor_tensor(count[:], route[:, 1, :], route[:, 2, :], ALU.add).then_inc(counted, 1)
                elif n == 19:
                    dve.tensor_tensor(pick[:, 2:3], pick[:, 1:2], pick[:, 0:1], ALU.subtract).then_inc(diff_ready, 1)
                elif n == 20:
                    dve.wait_ge(ratio_ready, b + 1)
                    done(dve.tensor_scalar(pick[:, 4:5], pick[:, 3:4], 1.0, None, ALU.add))
                elif n == 21:
                    after(17)
                    done(dve.reciprocal(pick[:, 5:6], pick[:, 4:5]))
                elif n == 22:
                    after(18)
                    done(dve.tensor_tensor(choice[:, par, 0, D:D + 1], pick[:, 5:6], g_tanh[:, 1:2], ALU.mult))
                elif n == 23:
                    after(19)
                    done(dve.tensor_tensor(choice[:, par, 1, D:D + 1], choice[:, par, 0, D:D + 1], pick[:, 3:4],
                                           ALU.mult))
                elif n == 24:
                    dve.wait_ge(spots_ready, b + 1)
                    done(dve.tensor_tensor(route[:, 5, :], spots[0:NQ, 0:E], run[0:NQ, :], ALU.add))
                elif n == 25:
                    after(21)
                    done(dve.tensor_tensor(run[:], run[:], spots[:, E:2 * E], ALU.add))
                elif n in (26, 27):
                    done(dve.tensor_tensor(route[:, n - 20, :], route[:, n - 25, :], route[:, 5, :], ALU.mult))
                elif n in (28, 29):
                    after(n - 5)
                    if not isinstance(b, int) or b >= 1:
                        dve.wait_ge(places_ready, 2 * b)
                    done(dve.tensor_reduce(pick[:, n - 22:n - 21], route[:, n - 22, :], AX.X, ALU.add))
                elif n in (30, 31):
                    after(n - 5)
                    dve.tensor_copy(place[:, par, n - 30:n - 29], pick[:, n - 24:n - 23]).then_inc(places_ready, 1)

            dve.wait_ge(const_in, DMA * 10)
            step(dve.tensor_copy(run[:], const("region")))
            dve.wait_ge(cleared, 6)
            dve.wait_ge(tanh_done, 1)
            used = [0]

            def bank_of(u, use, kinds):
                before = sum(k in kinds for units in PLAN[:u] for k, _, _ in units)
                return RING + (used[0] + before + [x for x in PLAN[u] if x[0] in kinds].index(use)) % 3

            def take(kind, b, par, n, bank):
                if kind in "st":
                    take_max(b, par, n, bank)
                elif kind == "m":
                    part_max(b, bank)
                elif kind == "o":
                    divide(b, bank)
                elif kind == "y":
                    add_y(b, bank)

            for n_use, (kind, b, n) in enumerate(FIRST):
                take(kind, b, b % 2, n, RING + n_use % 3)
                if kind == "s" and n == SM - 1:
                    join_max(b, b % 2)
            used[0] = len(FIRST)

            def body(i, it, par, kinds, before):
                def steps_for(chain, n):
                    if chain == "n" and "n" in kinds:
                        second_norm(i - 1, it + (par - 1) // 2, 1 - par, n)
                    elif chain == "r" and "c" in kinds:
                        routing(i - 2, par, n)

                for u in range(UNITS):
                    uses = [use for use in PLAN[u] if use[0] in kinds and use[0] not in "kvnrc"]
                    for n_use in range(max(len(uses), len(STEPS[u]))):
                        if n_use < len(uses):
                            kind, off, n = uses[n_use]
                            take(kind, i + off, (par + off) % 2, n, bank_of(u, uses[n_use], kinds))
                            if (kind, n) == (("t", 0) if "t" in kinds else ("s", SM - 1)):
                                join_max(i + 1, 1 - par)
                        if n_use < len(STEPS[u]):
                            steps_for(*STEPS[u][n_use])
                used[0] += len(uses_of(kinds))

            batches(dve, body)
            for n in ROUTE_1:
                routing(B - 2, 0, n)
            for n_use, (kind, b) in enumerate(TAIL):
                take(kind, b, b % 2, 0, RING + (used[0] + n_use) % 3)
                if kind == "c":
                    for n in ROUTE_2:
                        routing(b, b % 2, n)
                    if b == B - 2:
                        dve.wait_ge(rt_step, (B - 1) * RT_STEPS)
                        dve.tensor_tensor(fill_place[:].rearrange("p (n e) -> p n e", e=E),
                                          run[:].unsqueeze(1).to_broadcast([128, 2, E]),
                                          const("fill").rearrange("p (n e) -> p n e", e=E), ALU.add) \
                            .then_inc(fill_ready, 1)
                elif kind == "y":
                    for n in NORM:
                        second_norm(b, b // 2, b % 2, n)
                elif kind == "r":
                    for n in ROUTE_1:
                        routing(b, b % 2, n)
            dve.wait_ge(rt_step, B * RT_STEPS)
            step(dve.tensor_tensor(route[0:1, 7, :], run[0:1, :], const("region", 1), ALU.subtract))
            step(dve.tensor_tensor(is_full, route[0:1, 7, :].unsqueeze(2).to_broadcast([1, E, FULL]),
                                   const("full", 1).rearrange("q (e j) -> q e j", e=E), ALU.is_gt))
            step(dve.tensor_reduce(e_tiles, is_full, AX.X, ALU.add))
            step(dve.tensor_tensor(partial, e_tiles.unsqueeze(1).to_broadcast([1, E, E]),
                                   const("upto", 1).rearrange("q (e j) -> q e j", e=E), ALU.mult))
            step(dve.tensor_reduce(e_end, partial, AX.X, ALU.add))
            step(dve.tensor_scalar(e_jump, e_tiles, -128.0, float(REGION), ALU.mult, ALU.add))
            over_t = [1, TILES, E]
            step(dve.tensor_scalar(expert_of, const("rows", 1), 1.0 / 128, None, ALU.mult))
            step(dve.tensor_tensor(past_end, expert_of.unsqueeze(2).to_broadcast(over_t),
                                   e_end.unsqueeze(1).to_broadcast(over_t), ALU.is_ge))
            step(dve.tensor_tensor(past_jump, past_end, e_jump.unsqueeze(1).to_broadcast(over_t), ALU.mult))
            step(dve.tensor_reduce(jumped, past_jump, AX.X, ALU.add))
            dve.tensor_tensor(table[:, 0, :], jumped, const("rows", 1), ALU.add).then_inc(table_ready, 1)
            step(dve.tensor_reduce(row_of, past_end, AX.X, ALU.add))
            dve.tensor_scalar(table[:, 1, :], row_of, float(E - 1), None, ALU.min).then_inc(table_ready, 1)

            def take_dest(s, turn, slot):
                dve.wait_ge(t_row_in[slot], (turn + 1) * DMA)
                if not isinstance(s, int) or s >= SLOTS:
                    dve.wait_ge(t_y_out[slot], turn * DMA)
                step(dve.tensor_copy(t_gate[:, slot:slot + 1], t_row[:, slot, D:D + 1]))
                dve.tensor_copy(t_dest[:, slot:slot + 1], t_row[:, slot, D + 1:D + 2]).then_inc(t_dest_ready, 1)

            def dve_tile(s, turn, slot, step, values):
                par = slot % 2
                if not isinstance(s, int) or s < TILES:
                    take_dest(s, turn, slot)
                    dve.wait_ge(t_silu_done, s + 1)
                    if not isinstance(s, int) or s >= 2:
                        dve.wait_ge(t_turned, s - 1)
                    dve.tensor_tensor(t_hid[:, par, :], t_silu[:, par, :], ps[:, 2 * par + 1, 0:F], ALU.mult) \
                        .then_inc(t_hid_ready, 1)
                if not isinstance(s, int) or s >= 2:
                    last = (slot + 2) % SLOTS
                    dve.wait_ge(t_y_made, s - 1)
                    dve.tensor_scalar(t_y[:, last, :], ps[:, 7, 0:D], t_gate[:, last:last + 1], None,
                                      ALU.mult).then_inc(t_y_ready, 1)

            tiles(dve, dve_tile, lag=2)

            for c in range(NCH):
                dve.wait_ge(y_back[c], 2 * DMA)
                for n in (0, 1):
                    at_ = slice(c * CB * D, (c + 1) * CB * D)
                    if n:
                        dve.wait_ge(added, 2 * c + 1)
                    dve.tensor_tensor(xs[:, at_], xs[:, at_], y_in[n][:, at_], ALU.add).then_inc(added, 1)

        @block.tensor
        def _(pe):
            def turn_chunk(c):
                pe.wait_ge(xn_ready, c + 1)
                if c >= 2:
                    pe.wait_ge(xt_ready, c - 1)
                for t in range(CB):
                    mm = pe.transpose(ps[:, c % 2, t * NQ:(t + 1) * NQ], xn[:, c % 2, t * D:(t + 1) * D],
                                      idn[0:NQ, 0:NQ])
                mm.then_inc(xn_turned, 1)

            def make_q(c):
                pe.wait_ge(xt_ready, c + 1)
                if c >= 2:
                    pe.wait_ge(q_scaled, c - 1)
                pe.matmul(ps[:, 2 + c % 2, 0:CT], wq[:], xt[:, c * CT:(c + 1) * CT], start=True, stop=True) \
                    .then_inc(q_made, 1)

            def make_k(b, it, par, n, bank):
                if n == 0:
                    pe.wait_ge(ctx_in[par], (it + 1) * DMA)
                pe.matmul(ps[:, bank, 0:CH[n]], wk[:], ctx[:, par, CO[n]:CO[n] + CH[n]], start=True, stop=True) \
                    .then_inc(k_made, 1)

            def make_v(par, n, bank):
                for t in range(4 * n, 4 * n + 4):
                    r = key_rows(t)
                    mm = pe.matmul(ps[0:r, bank, (t % 4) * D:(t % 4 + 1) * D], ctx[:, par, t * 128:t * 128 + r],
                                   wv[:], start=True, stop=True)
                mm.then_inc(v_made, 1)

            def make_scores(b, par, n, bank):
                t, c = n // NC, n % NC
                r = score_rows(t)
                if t == 0:
                    pe.wait_ge(k_taken, b * NC + c + 1)
                if n == 0:
                    pe.wait_ge(block_ready, b + 1)
                rows = q_block[:, par, :, :].rearrange("p h n -> p (h n)")[:, t * 128:t * 128 + r]
                pe.matmul(ps[0:r, bank, 0:CH[c]], rows, k_hi[:, par, CO[c]:CO[c] + CH[c]],
                          start=True, stop=True).then_inc(sm_made, 1)

            def turn_max(b, bank):
                pe.wait_ge(neg_ready, b + 1)
                pe.transpose(ps[0:RT, bank, 0:128], neg_max[:], idn[:]).then_inc(max_turned, 1)

            def gather(b, bank):
                pe.wait_ge(o_copied, b + 1)
                for pick_, at_ in ((pden, 0), (pnum, 128)):
                    for n in range(4):
                        mm = pe.matmul(ps[:, bank, at_:at_ + NQ], pick_[:, n, :], o_sum[:, n * NQ:(n + 1) * NQ],
                                       start=(n == 0), stop=(n == 3))
                mm.then_inc(nd_made, 1)

            def make_y(b, bank):
                pe.wait_ge(on_ready, b + 1)
                pe.matmul(ps[0:NQ, bank, 0:D], o_norm[:], wo[:], start=True, stop=True).then_inc(y_made, 1)

            def turn_norm(b, par, bank):
                pe.wait_ge(norm_ready, b + 1)
                pe.transpose(ps[:, bank, 0:NQ], choice[:, par, 0, 0:D], idn[0:NQ, 0:NQ]).then_inc(x2_turned, 1)

            def mix(b, bank):
                pe.wait_ge(x2_ready, b + 1)
                pe.matmul(ps[0:NQ, bank, 0:3 * E], x_turned[:], wr[:], start=True, stop=True).then_inc(mixed_made, 1)

            def count_before(b, bank):
                pe.wait_ge(counted, b + 1)
                pe.matmul(ps[:, bank, 0:E], const("before", NQ), count[:], start=True, stop=True)
                pe.matmul(ps[:, bank, E:2 * E], const("ones", NQ), count[:], start=True, stop=True) \
                    .then_inc(spots_made, 1)

            def make(kind, b, it, par, n, bank):
                if kind in "st":
                    make_scores(b, par, n, bank)
                elif kind == "k":
                    make_k(b, it, par, n, bank)
                elif kind == "v":
                    make_v(par, n, bank)
                elif kind == "m":
                    turn_max(b, bank)
                elif kind == "o":
                    gather(b, bank)
                elif kind == "y":
                    make_y(b, bank)
                elif kind == "n":
                    turn_norm(b, par, bank)
                elif kind == "r":
                    mix(b, bank)
                else:
                    count_before(b, bank)

            used = [0]
            pe.wait_ge(first_in, DMA * 3)
            for n_use, (kind, b, n) in enumerate(FIRST):
                if n_use == NC:
                    for c in range(NCH):
                        turn_chunk(c)
                        if c >= 1:
                            make_q(c - 1)
                    make_q(NCH - 1)
                if n_use >= 3:
                    ring_read(pe, *FIRST[n_use - 3])
                if n_use == NC:
                    pe.wait_ge(const_in, DMA * 10)
                make(kind, b, 0, b % 2, n, RING + n_use % 3)
            used[0] = len(FIRST)

            def scores(i, par, u):
                t, half = u // 2, u % 2
                r = key_rows(t)
                if u == 0:
                    pe.wait_ge(k_in, (i + 1) * COPIES * DMA)
                    pe.wait_ge(q_in, (i + 1) * COPIES * DMA)
                    pe.wait_ge(max_in, (i + 1) * 2 * DMA)
                if not isinstance(i, int) or i * UNITS + u >= 2:
                    pe.wait_ge(exp_done, i * UNITS + u - 1)
                for n in range(4):
                    hp = 4 * half + n
                    mm = pe.matmul(ps[0:r, 2 * (u % 2) + n // 2, (n % 2) * PW:(n % 2 + 1) * PW],
                                   k_stack[0:KROWS, par, hp, t * 128:t * 128 + r],
                                   q_stack[0:KROWS, par, hp * PW:(hp + 1) * PW], start=True, stop=True)
                mm.then_inc(st_made, 1)

            def product(i, par, u):
                t, half = u // 2, u % 2
                pe.wait_ge(exp_done, i * UNITS + u + 1)
                if u == 0:
                    pe.wait_ge(v_taken, (i + 1) * NC)
                    if not isinstance(i, int) or i >= 1:
                        pe.wait_ge(o_copied, i)
                for n in range(4):
                    mm = pe.matmul(ps[32 * n:32 * n + 32, OB, half * PW:(half + 1) * PW],
                                   v_ones[:, par, t, 4 * half + n, :], probs[:, u % 4, n * PW:(n + 1) * PW],
                                   start=(u == 0), stop=(t == KT - 1), skip_group_check=True)
                mm.then_inc(pv_done, 1)

            def body(i, it, par, kinds, before):
                uses = uses_of(kinds)
                past = [(k, o - 1, n) for k, o, n in uses_of(before)[-3:]] if before else \
                    [(k, o, n) for k, o, n in FIRST[-3:]]
                line = past + uses
                if len(line) < len(past) + 1:
                    line = past
                at_use = [3]
                for u in range(UNITS):
                    scores(i, par, u)
                    if u >= 2:
                        product(i, par, u - 2)
                    elif not isinstance(i, int) or i >= 1:
                        product(i - 1, 1 - par, UNITS - 2 + u)
                    for kind, off, n in PLAN[u]:
                        if kind in kinds:
                            k_, o_, n_ = line[at_use[0] - 3]
                            ring_read(pe, k_, i + o_, n_)
                            make(kind, i + off, it + 1, par if kind in "kt" else 1 - par, n, RING + used[0] % 3)
                            at_use[0] += 1
                            used[0] += 1

            batches(pe, body)
            for u in (UNITS - 2, UNITS - 1):
                product(B - 1, 1, u)
            past = [(kind, B - 1 + off) for kind, off, n in uses_of(kinds_of(B - 1))][-3:]
            for n_use, (kind, b) in enumerate(TAIL):
                before = (past + TAIL)[n_use]
                ring_read(pe, *before, 0)
                make(kind, b, 0, b % 2, 0, RING + (used[0] + n_use) % 3)

            pe.wait_ge(w_in, (1 + len(FT)) * DMA)
            pe.wait_ge(table_ready, 2)

            def expert(values, s, key):
                if key not in values:
                    values[key] = pe.value_load(table[0:1, 1, bass.ds(s, 1)], min_val=0, max_val=E - 1)
                return values[key]

            def turn_x(s, turn, slot):
                pe.wait_ge(t_row_in[slot], (turn + 1) * DMA)
                if not isinstance(s, int) or s >= 1:
                    pe.wait_ge(t_x_ready, s)
                pe.transpose(ps[:, 6, 0:128], t_row[:, slot, 0:D], idn[:]).then_inc(t_x_turned, 1)

            def pe_tile(s, turn, slot, step, values):
                par = slot % 2
                if isinstance(s, int) and s == 0:
                    turn_x(0, 0, 0)
                if not isinstance(s, int) or s + 1 < TILES:
                    turn_x(s + 1, turn + (slot + 1) // SLOTS, (slot + 1) % SLOTS)
                if not isinstance(s, int) or s < TILES:
                    e = expert(values, s, step)
                    pe.wait_ge(t_x_ready, s + 1)
                    if not isinstance(s, int) or s >= 2:
                        pe.wait_ge(t_hid_ready, s - 1)
                    for n in (0, 1):
                        mm = pe.matmul(ps[:, 2 * par + n, 0:F], t_x[:, par, :],
                                       w1[:, bass.ds(e * (2 * F) + n * F, F)], start=True, stop=True)
                    mm.then_inc(t_h_made, 1)
                if not isinstance(s, int) or s >= 2:
                    e = expert(values, s - 2, step - 2)
                    pe.wait_ge(t_turn_ready, s - 1)
                    if not isinstance(s, int) or s >= 3:
                        pe.wait_ge(t_y_ready, s - 2)
                    for t, (f0, fr) in enumerate(FT):
                        mm = pe.matmul(ps[:, 7, 0:D], t_turn[0:fr, par, t * 128:(t + 1) * 128],
                                       k_flat[0:fr, bass.ds(e * (len(FT) * D) + (half + t * D), D)],
                                       start=(t == 0), stop=(t == len(FT) - 1))
                    mm.then_inc(t_y_made, 1)
                if not isinstance(s, int) or 1 <= s <= TILES:
                    pe.wait_ge(t_hid_ready, s)
                    if not isinstance(s, int) or s >= 3:
                        pe.wait_ge(t_turn_ready, s - 2)
                    for t, (f0, fr) in enumerate(FT):
                        mm = pe.transpose(ps[0:fr, 5 - par, t * 128:(t + 1) * 128], t_hid[:, 1 - par, f0:f0 + fr],
                                          idn[:])
                    mm.then_inc(t_turned, 1)

            tiles(pe, pe_tile, lag=2)


_OUT = (B, NQ, D)


def kernel(x, ctx_512, g_xattn, g_ffn, L0_xattn_Wq, L0_xattn_Wkv, L0_xattn_Wo, L0_ffn_wqkv, L0_ffn_w1, L0_ffn_w2):
    import concourse.bacc as _bacc
    from concourse.bass_utils import run_bass_kernel_spmd as _run

    def turned(a, *axes):
        return np.ascontiguousarray(np.transpose(a, axes or None))

    order = np.arange(D).reshape(NP, 2, HD).transpose(1, 2, 0).reshape(D)
    num = np.zeros((128, 4, 128), np.float32)
    den = np.zeros((128, 4, 128), np.float32)
    for h in range(H):
        hp, u = h // 2, h % 2
        for d in range(HD):
            num[32 * (hp % 4) + HD * u + d, 2 * (hp // 4) + u, HD * h + d] = 1
            den[32 * (hp % 4) + 16 + HD * u + d, 2 * (hp // 4) + u, HD * h + d] = 1
    mask = np.zeros((D, H), mybir.dt.np(BF16) if hasattr(mybir.dt, "np") else np.float32)
    for p, channel in enumerate(order):
        mask[p, channel // HD] = 1
    pack = {name: np.zeros((128, z - a), np.float32) for name, (a, z) in PACK.items()}
    part = np.arange(128)
    pack["before"][:] = part[:, None] < part
    pack["ones"][:] = 1
    pack["region"][:] = REGION * np.arange(E)
    pack["fill"][:] = part[:, None] + 128 * (np.arange(2 * E) // E)
    pack["root"][:] = -0.5
    pack["spare"][:] = 2 * TOK + 128 * np.arange(E + SPARE) + part[:, None]
    pack["token"][:NQ] = (np.arange(2) * TOK + NQ * np.arange(B)[:, None]).reshape(-1) + part[:NQ, None]
    pack["rows"][:] = 128 * np.arange(TILES)
    pack["full"][:] = np.tile(128 * np.arange(FULL), E)
    pack["upto"][:] = np.tril(np.ones((E, E))).reshape(-1)
    x, wkv = np.asarray(x), np.asarray(L0_xattn_Wkv)
    arrays = {
        "x": np.ascontiguousarray(x),
        "ctx_t": turned(np.asarray(ctx_512), 0, 2, 1),
        "g_x": np.asarray(g_xattn), "g_f": np.asarray(g_ffn),
        "wq_t": turned(np.asarray(L0_xattn_Wq)[order]),
        "wk_t": turned(wkv[:D][order]),
        "wv_t": turned(wkv[D:]),
        "wo_t": turned(np.asarray(L0_xattn_Wo)),
        "wr_t": turned(np.asarray(L0_ffn_wqkv)),
        "w1_t": turned(np.asarray(L0_ffn_w1), 2, 0, 1).reshape(D, E * 2 * F),
        "w2_t": turned(np.asarray(L0_ffn_w2), 0, 2, 1),
        "ident": np.eye(128, dtype=np.float32),
        "head_mask": mask,
        "pick_num": num,
        "pick_den": den,
        "rank": np.tile(np.arange(E, 0, -1, dtype=np.float32), (NQ, 1)),
        "pack": np.concatenate(list(pack.values()), axis=1),
    }
    nc = _bacc.Bacc("TRN2", target_bir_lowering=False, num_devices=1)
    args = [nc.dram_tensor(f"in_{k}", a.shape, mybir.dt.from_np(a.dtype), kind="ExternalInput").ap()
            for k, a in arrays.items()]
    args.append(nc.dram_tensor("out", _OUT, F32, kind="ExternalOutput").ap())
    build(nc, *args)
    r = _run(nc, [{f"in_{k}": a for k, a in arrays.items()}], core_ids=[0])
    return r.results[0]["out"]
```
